# Optimizing a Trainium2 kernel written in Bass

```python
import numpy as np
import jax
import jax.numpy as jnp

def _softmax(x, axis=-1):
    return jax.nn.softmax(x, axis=axis)

def _gelu(x):
    return jax.nn.gelu(x, approximate=True)

def _silu(x):
    return jax.nn.silu(x)

def _sigmoid(x):
    return jax.nn.sigmoid(x)

def _layernorm(x, axis=-1, eps=1e-05):
    m = jnp.mean(x, axis=axis, keepdims=True)
    v = jnp.var(x, axis=axis, keepdims=True)
    return (x - m) / jnp.sqrt(v + eps)

def _scatter_add(tgt, idx, src, axis=0):
    return tgt.at[idx].add(src)

def _segment_sum(src, seg, n):
    return jax.ops.segment_sum(src, seg, n)
kernel_name = 'mk_flamingo_gated_d1_seqx_r8_1a69ce'

def setup_inputs(seed: int=0):
    np.random.seed(seed)
    _w = jnp.asarray

    def _rec_inputs():
        import jax
        import jax.numpy as jnp
        _rk = jax.random.key(seed)
        x = 7.22e-05 + 1 * jax.random.normal(jax.random.fold_in(_rk, 1), (128, 64, 128), jnp.float32)
        _lenS = 64 - jax.random.randint(jax.random.fold_in(_rk, 7), (128,), 0, max(1, 64 // 4) + 1, jnp.int32)
        _lenS2 = 64 - jax.random.randint(jax.random.fold_in(_rk, 8), (128,), 0, max(1, 64 // 4) + 1, jnp.int32)
        _ctx_768P = jax.random.normal(jax.random.fold_in(_rk, 11), (128, 16, 96), jnp.float32)
        _ctx_768c = jax.random.dirichlet(jax.random.fold_in(_rk, 511), 0.3 * jnp.ones((16,), jnp.float32), (128, 64))
        _ctx_768t = jnp.einsum('bsk,bkd->bsd', _ctx_768c, _ctx_768P)
        _ctx_768t = _ctx_768t * jax.lax.rsqrt(jnp.mean(jnp.square(_ctx_768t)) + 1e-12) * 0.953939
        ctx_768 = -0.000191848 + 0.999787 * (_ctx_768t + 0.3 * jax.random.normal(jax.random.fold_in(_rk, 611), (128, 64, 96), jnp.float32))
        _g = jax.random.normal(jax.random.fold_in(_rk, 9001), (2, 1), jnp.float32)
        _g = jnp.sign(_g) * jnp.maximum(jnp.abs(_g), 1.0) + (_g == 0) * 1.0
        g_xattn = _g[0]
        g_ffn = _g[1]
        return (x, ctx_768, g_xattn, g_ffn)
    x, ctx_768, g_xattn, g_ffn = _rec_inputs()

    def _L0_xattn_setup():
        import jax, jax.numpy as jnp
        import numpy as np
        DIM = 128
        CTX_DIM = 96
        H = 16
        DH = 64
        INNER = H * DH
        EPS = 1e-05

        def layer_norm(x, gamma, beta):
            mu = jnp.mean(x, axis=-1, keepdims=True)
            var = jnp.mean(jnp.square(x - mu), axis=-1, keepdims=True)
            return (x - mu) * jax.lax.rsqrt(var + EPS) * gamma + beta
        key = jax.random.key(seed)
        ks = jax.random.split(key, 8)
        B, N, M = (4, 256, 256)
        x = jax.random.normal(ks[0], (B, N, DIM), dtype=jnp.float32)
        context = jax.random.normal(ks[1], (B, M, CTX_DIM), dtype=jnp.float32)
        g_x = jnp.ones((DIM,), jnp.float32)
        b_x = jnp.zeros((DIM,), jnp.float32)
        g_c = jnp.ones((CTX_DIM,), jnp.float32)
        b_c = jnp.zeros((CTX_DIM,), jnp.float32)
        Wq = jax.random.normal(ks[2], (DIM, INNER), dtype=jnp.float32) / np.sqrt(DIM)
        Wk = jax.random.normal(ks[3], (CTX_DIM, INNER), dtype=jnp.float32) / np.sqrt(CTX_DIM)
        Wv = jax.random.normal(ks[4], (CTX_DIM, INNER), dtype=jnp.float32) / np.sqrt(CTX_DIM)
        Wo = jax.random.normal(ks[5], (INNER, DIM), dtype=jnp.float32) / np.sqrt(INNER)
        return {'x': x, 'context': context, 'g_x': g_x, 'b_x': b_x, 'g_c': g_c, 'b_c': b_c, 'Wq': Wq, 'Wk': Wk, 'Wv': Wv, 'Wo': Wo}
    _L0_xattn_all = _L0_xattn_setup()
    _L0_xattn_in = {k: v for k, v in _L0_xattn_all.items() if k in ('g_x', 'b_x', 'g_c', 'b_c', 'Wq', 'Wk', 'Wv', 'Wo')}
    del _L0_xattn_all

    def _L0_ffn_setup():
        import jax, jax.numpy as jnp
        import numpy as np
        B, S, D, E, F = (2, 256, 128, 14, 256)
        key = jax.random.key(seed)
        k = jax.random.split(key, 4)
        h = jax.random.normal(k[0], (B, S, D), dtype=jnp.float32)
        router_w = jax.random.normal(k[1], (D, E), dtype=jnp.float32) * 0.02
        w1 = jax.random.uniform(k[2], (E, D, F), dtype=jnp.float32, minval=-1.0, maxval=1.0) * float(np.sqrt(6.0 / D))
        w2 = jax.random.uniform(k[3], (E, F, D), dtype=jnp.float32, minval=-1.0, maxval=1.0) * float(np.sqrt(6.0 / F))
        b1 = jnp.zeros((E, F), dtype=jnp.float32)
        b2 = jnp.zeros((E, D), dtype=jnp.float32)
        return {'h': h, 'router_w': router_w, 'w1': w1, 'b1': b1, 'w2': w2, 'b2': b2}
    _L0_ffn_all = _L0_ffn_setup()
    _L0_ffn_in = {k: v for k, v in _L0_ffn_all.items() if k in ('router_w', 'w1', 'b1', 'w2', 'b2')}
    del _L0_ffn_all
    return {'x': x, 'ctx_768': ctx_768, 'g_xattn': g_xattn, 'g_ffn': g_ffn, 'L0_xattn_g_x': _L0_xattn_in['g_x'], 'L0_xattn_b_x': _L0_xattn_in['b_x'], 'L0_xattn_g_c': _L0_xattn_in['g_c'], 'L0_xattn_b_c': _L0_xattn_in['b_c'], 'L0_xattn_Wq': _L0_xattn_in['Wq'], 'L0_xattn_Wk': _L0_xattn_in['Wk'], 'L0_xattn_Wv': _L0_xattn_in['Wv'], 'L0_xattn_Wo': _L0_xattn_in['Wo'], 'L0_ffn_router_w': _L0_ffn_in['router_w'], 'L0_ffn_w1': _L0_ffn_in['w1'], 'L0_ffn_b1': _L0_ffn_in['b1'], 'L0_ffn_w2': _L0_ffn_in['w2'], 'L0_ffn_b2': _L0_ffn_in['b2']}

def reference(x, ctx_768, g_xattn, g_ffn, L0_xattn_g_x, L0_xattn_b_x, L0_xattn_g_c, L0_xattn_b_c, L0_xattn_Wq, L0_xattn_Wk, L0_xattn_Wv, L0_xattn_Wo, L0_ffn_router_w, L0_ffn_w1, L0_ffn_b1, L0_ffn_w2, L0_ffn_b2):
    import jax
    import jax.numpy as jnp

    def _L0_xattn_ref(x, context, g_x, b_x, g_c, b_c, Wq, Wk, Wv, Wo):
        import jax, jax.numpy as jnp
        import numpy as np
        DIM = 128
        CTX_DIM = 96
        H = 16
        DH = 64
        INNER = H * DH
        EPS = 1e-05

        def layer_norm(x, gamma, beta):
            mu = jnp.mean(x, axis=-1, keepdims=True)
            var = jnp.mean(jnp.square(x - mu), axis=-1, keepdims=True)
            return (x - mu) * jax.lax.rsqrt(var + EPS) * gamma + beta
        B, N, _ = x.shape
        M = context.shape[1]
        xn = layer_norm(x, g_x, b_x)
        cn = layer_norm(context, g_c, b_c)
        q = (xn @ Wq).reshape(B, N, H, DH).transpose(0, 2, 1, 3)
        k = (cn @ Wk).reshape(B, M, H, DH).transpose(0, 2, 1, 3)
        v = (cn @ Wv).reshape(B, M, H, DH).transpose(0, 2, 1, 3)
        scale = jnp.float32(1.0 / np.sqrt(DH))
        sim = jnp.einsum('bhid,bhjd->bhij', q, k) * scale
        attn = jax.nn.softmax(sim, axis=-1)
        out = jnp.einsum('bhij,bhjd->bhid', attn, v)
        out = out.transpose(0, 2, 1, 3).reshape(B, N, INNER)
        return out @ Wo

    def _L0_ffn_ref(h, router_w, w1, b1, w2, b2):
        import jax, jax.numpy as jnp
        import numpy as np
        B, S, D, E, F = (2, 256, 128, 14, 256)
        Bb, Ss, Dd = h.shape
        x = h.reshape(-1, Dd)
        logits = x @ router_w
        assignments = jnp.argmax(logits, axis=-1)
        probs = jax.nn.softmax(logits, axis=-1)
        weights = jnp.take_along_axis(probs, assignments[:, None], axis=1)[:, 0]
        hid = jnp.einsum('nd,edf->nef', x, w1) + b1
        hid = jax.nn.gelu(hid, approximate=False)
        all_out = jnp.einsum('nef,efd->ned', hid, w2) + b2
        sel = jnp.take_along_axis(all_out, assignments[:, None, None], axis=1)[:, 0, :]
        moe_out = (sel * weights[:, None]).reshape(Bb, Ss, Dd)
        return moe_out
    x = x + jnp.tanh(g_xattn[0]) * _L0_xattn_ref(_layernorm(x, axis=-1), ctx_768, L0_xattn_g_x, L0_xattn_b_x, L0_xattn_g_c, L0_xattn_b_c, L0_xattn_Wq, L0_xattn_Wk, L0_xattn_Wv, L0_xattn_Wo)
    x = x + jnp.tanh(g_ffn[0]) * _L0_ffn_ref(_layernorm(x, axis=-1), L0_ffn_router_w, L0_ffn_w1, L0_ffn_b1, L0_ffn_w2, L0_ffn_b2)
    return x

_drawn_inputs = setup_inputs


def setup_inputs(seed=0):
    import zlib

    import numpy as np

    out = dict(_drawn_inputs(seed))
    spreads = {'L0_xattn_g_x': (1.0, 0.2),
     'L0_xattn_b_x': (0.0, 0.311),
     'L0_xattn_g_c': (1.0, 0.2),
     'L0_xattn_b_c': (0.0, 0.1),
     'L0_ffn_b1': (0.0, 0.8),
     'L0_ffn_b2': (0.0, 0.8)}
    factors = {}
    for name, (base, spread) in spreads.items():
        noise = np.random.default_rng([zlib.crc32(name.encode()), seed]).standard_normal(out[name].shape)
        drawn = base * np.exp(spread * noise) if base else spread * noise
        out[name] = jnp.asarray(drawn.astype(out[name].dtype))
    for name, factor in factors.items():
        out[name] = (out[name] * factor).astype(out[name].dtype)
    return out
```

```python
from contextlib import ExitStack

import concourse.bass as bass
from concourse import mybir

F32 = mybir.dt.float32
F32R = mybir.dt.float32r
BF16 = mybir.dt.bfloat16
I32 = mybir.dt.int32
ALU = mybir.AluOpType
ACT = mybir.ActivationFunctionType
AX = mybir.AxisListType

P = 128
SEQ = 64
DH = 64
EPS = 1e-5
SCALE = float(DH) ** -0.5
RSQRT_SEED = float(0x5F3759DF)
NEWTON = 3
LOOP_FROM, LOOP_TO = 2, 14
RING = 8


def gated_block_kernel(nc, x, ctx768, g_xattn, g_ffn, g_x, b_x, g_c, b_c, Wq, Wk, Wv, Wo,
                       router_w, w1, b1, w2, b2, out):
    B, N, D = x.shape
    C = ctx768.shape[2]
    INNER = Wq.shape[1]
    H = INNER // DH
    M8 = INNER // P
    HG = H // 4
    E, _, F = w1.shape
    FK = F // P
    TOK = B * N
    GT = 2 * P
    GROUPS = TOK // GT
    PAIRS = TOK // P
    REGION = TOK + P
    ROW = D + D + 2
    TILES = -(-(TOK // P + E - 1) // RING) * RING
    assert N == SEQ and D == P and GROUPS == 2 * (LOOP_TO + 2)

    rows_dram = nc.dram_tensor("rows_by_expert", [E * REGION + P, ROW], F32, kind="Internal").ap()

    x_t = x.rearrange("b n d -> (b n) d").rearrange("(g j p) d -> g p j d", j=2, p=P)
    c_t = ctx768.rearrange("b n d -> (b n) d").rearrange("(g j p) d -> g p j d", j=2, p=P)
    out_rows = out.rearrange("b n d -> (b n) d")

    with ExitStack() as stack:
        def sb(name, shape, dt=F32):
            return stack.enter_context(nc.sbuf_tensor(name, shape, dt))

        def psum(name, shape):
            return stack.enter_context(nc.psum_tensor(name, shape, F32))

        def sem(name):
            return stack.enter_context(nc.semaphore(name))

        Wq_h, Wq_l = sb("Wq_h", [P, INNER], F32R), sb("Wq_l", [P, INNER], F32R)
        Wk_h, Wk_l = sb("Wk_h", [C, INNER], F32R), sb("Wk_l", [C, INNER], F32R)
        Wv_h, Wv_l = sb("Wv_h", [C, INNER], F32R), sb("Wv_l", [C, INNER], F32R)
        Wo_h, Wo_l = sb("Wo_h", [P, M8, D], F32R), sb("Wo_l", [P, M8, D], F32R)
        w1_sb = sb("w1_sb", [P, E * F])
        w2_sb = sb("w2_sb", [P, E * F])
        rw_sb = sb("rw_sb", [P, E])
        gx_col, bx_col = sb("gx_col", [P, 1]), sb("bx_col", [P, 1])
        gc_col, bc_col = sb("gc_col", [C, 1]), sb("bc_col", [C, 1])
        gates = sb("gates", [P, 2])
        tanhs = sb("tanhs", [P, 2])
        ident = sb("ident", [P, P])
        before = sb("before", [P, P], BF16)
        ones_b = sb("ones_b", [P, P], BF16)
        zero1 = sb("zero1", [P, 1])
        var_mul, var_add = sb("var_mul", [P, 6]), sb("var_add", [P, 6])
        e_int, e_iota = sb("e_int", [P, 2, E], I32), sb("e_iota", [P, 2, E])
        r_int = sb("r_int", [P, E], I32)
        token = sb("token", [P, 2], I32)
        token_step = sb("token_step", [P, 2], I32)
        x_in, c_in = sb("x_in", [P, 2, 2, D]), sb("c_in", [P, 2, 2, C])
        x_res = sb("x_res", [P, 2, 2, D])
        zx, zc = sb("zx", [P, 2, D]), sb("zc", [P, 2, C])
        xf, cf = sb("xf", [P, GT]), sb("cf", [C, GT])
        XT_h, XT_l = sb("XT_h", [P, 2, GT], F32R), sb("XT_l", [P, 2, GT], F32R)
        CT_h, CT_l = sb("CT_h", [C, 2, GT], F32R), sb("CT_l", [C, 2, GT], F32R)
        QT, KT = sb("QT", [P, 2, M8, GT]), sb("KT", [P, 2, M8, GT])
        V = sb("V", [P, 2, 2, INNER])
        probs = sb("probs", [P, 2, 2 * HG * 2, SEQ])
        row_max, row_sum, row_inv = sb("row_max", [P, 16]), sb("row_sum", [P, 16]), sb("row_inv", [P, 16])
        PTs = sb("PTs", [P, 2, 4 * P])
        OT_h, OT_l = sb("OT_h", [P, M8, GT], F32R), sb("OT_l", [P, M8, GT], F32R)
        aT = sb("aT", [P, GT])
        rows = sb("rows", [P, 2, 2, ROW])
        n2T = sb("n2T", [P, GT])
        bn6 = sb("bn6", [P, 6, 6])
        mv = sb("mv", [P, 6, 2])
        nw, nq = sb("nw", [P, 6]), sb("nq", [P, 6])
        rstd, shift = sb("rstd", [P, 6]), sb("shift", [P, 6])
        lmax = sb("lmax", [P, 2])
        dl, el, cand = sb("dl", [P, 2, E]), sb("el", [P, 2, E]), sb("cand", [P, 2, E])
        first, den, inv = sb("first", [P, 2]), sb("den", [P, 2]), sb("inv", [P, 2])
        onehot = sb("onehot", [P, 2, E], BF16)
        place = sb("place", [P, 2, E])
        place_i = sb("place_i", [P, 2, 2], I32)
        next_row = sb("next_row", [P, E])
        pad_row = sb("pad_row", [P, ROW])
        next_i = sb("next_i", [1, E], I32)
        ends_i = sb("ends_i", [1, E], I32)
        n_tiles, cum, one14 = sb("n_tiles", [1, E]), sb("cum", [1, E]), sb("one14", [1, E])
        t_int, t_f = sb("t_int", [1, TILES], I32), sb("t_f", [1, TILES])
        past = sb("past", [1, TILES, E])
        t_expert, t_start, t_row = sb("t_expert", [1, TILES]), sb("t_start", [1, TILES]), sb("t_row", [1, TILES])
        row_tab = sb("row_tab", [1, TILES], I32)
        f_tab = sb("f_tab", [1, TILES], I32)
        d_tab = sb("d_tab", [1, TILES], I32)

        QTf = QT[:, :, :, :].rearrange("p a m t -> p (a m t)")
        KTf = KT[:, :, :, :].rearrange("p a m t -> p (a m t)")
        Vf = V[:, :, :, :].rearrange("p a m t -> p (a m t)")
        HALF = M8 * GT
        raw_q, raw_k = QTf[:, HALF:HALF + INNER], QTf[0:C, HALF + INNER:HALF + 2 * INNER]
        raw_v, raw_o = KTf[0:C, HALF:HALF + INNER], KTf[:, HALF + INNER:HALF + 2 * INNER]
        b1_sb = QTf[:, 0:E * F]
        b2_sb = KTf[:, 0:E * D]
        at = E * D
        pre = [KTf[:, at + F * i:at + F * (i + 1)] for i in range(2)]
        at += 2 * F
        hid = [KTf[:, at + F * i:at + F * (i + 1)] for i in range(2)]
        at += 2 * F
        n2_T = [KTf[:, at + P * i:at + P * (i + 1)] for i in range(2)]
        tile_rows = [Vf[:, ROW * i:ROW * (i + 1)] for i in range(RING)]
        at = RING * ROW
        tile_out = [Vf[:, at + D * i:at + D * (i + 1)] for i in range(RING)]
        at += RING * D
        hid_T = [Vf[:, at + F * i:at + F * (i + 1)] for i in range(2)]
        ysum = sb("ysum", [P, D])

        psJ = [psum("psJ0", [P, 512]), psum("psJ1", [P, 512])]
        psM = psum("psM", [P, 512])
        psT = psum("psT", [P, 512])
        psS = psum("psS", [P, 1024])
        psO = psum("psO", [P, 1024])

        s_small, s_raw, s_ffn, s_bias = sem("s_small"), sem("s_raw"), sem("s_ffn"), sem("s_bias")
        s_in = [sem("s_in0"), sem("s_in1")]
        s_res = [sem("s_res0"), sem("s_res1")]
        s_const, s_cc, s_tanh = sem("s_const"), sem("s_cc"), sem("s_tanh")
        s_wh, s_wl = sem("s_wh"), sem("s_wl")
        s_stat = sem("s_stat")
        s_agg = sem("s_agg")
        s_stat2, s_agg2 = sem("s_stat2"), sem("s_agg2")
        s_newton = sem("s_newton")
        s_zm, s_z = sem("s_zm"), sem("s_z")
        s_prep, s_xf = sem("s_prep"), sem("s_xf")
        s_hi, s_lo = sem("s_hi"), sem("s_lo")
        s_job, s_jobev = sem("s_job"), sem("s_jobev")
        s_qk, s_max, s_sub, s_exp = sem("s_qk"), sem("s_max"), sem("s_sub"), sem("s_exp")
        s_sum, s_inv, s_norm = sem("s_sum"), sem("s_inv"), sem("s_norm")
        s_pt, s_ptev = sem("s_pt"), sem("s_ptev")
        s_pv, s_oh, s_ol = sem("s_pv"), sem("s_oh"), sem("s_ol")
        s_oproj, s_aT = sem("s_oproj"), sem("s_aT")
        s_posta, s_x2 = sem("s_posta"), sem("s_x2")
        s_n2m, s_n2 = sem("s_n2m"), sem("s_n2")
        s_postb, s_n2T = sem("s_postb"), sem("s_n2T")
        s_logit, s_lmax, s_dl, s_el = sem("s_logit"), sem("s_lmax"), sem("s_dl"), sem("s_el")
        s_route = sem("s_route")
        s_hot = sem("s_hot")
        s_rank, s_ranked = sem("s_rank"), sem("s_ranked")
        s_place = sem("s_place")
        s_id, s_tok = sem("s_id"), sem("s_tok")
        s_scat = [sem("s_scat0"), sem("s_scat1")]
        s_pad, s_dummy, s_tab = sem("s_pad"), sem("s_dummy"), sem("s_tab")
        f_load = [sem(f"f_load{i}") for i in range(RING)]
        f_scat = [sem(f"f_scat{i}") for i in range(RING)]
        f_t1, f_t1ev, f_w1, f_pre, f_gelu = sem("f_t1"), sem("f_t1ev"), sem("f_w1"), sem("f_pre"), sem("f_gelu")
        f_t2, f_t2ev, f_w2, f_sum, f_out = sem("f_t2"), sem("f_t2ev"), sem("f_w2"), sem("f_sum"), sem("f_out")
        f_send = sem("f_send")

        NEWT = 3 + 3 * NEWTON + 1
        N_SMALL = 10 * 16

        class Plan:

            def __init__(self, u, k, tail=False):
                self.k, self.j = k, k // 2
                self.odd = k % 2 == 1
                self.g = 2 * u + k // 2
                self.s = 4 * u + k
                self.u = u
                self.fixed = isinstance(u, int)

            def group(self, lag):
                g = self.g - lag
                if self.fixed and not 0 <= g < GROUPS:
                    return None
                return g

            def pair(self, lag):
                s = self.s - lag
                if self.fixed and not 0 <= s < PAIRS:
                    return None
                return s

            def par(self, lag=0):
                return (self.j - lag) % 2

            def uses(self, lag):
                return self.u + (self.j - lag - self.par(lag)) // 2 + 1

        STEPS_U = GROUPS // 2 + 2

        def run(eng, step):
            for u in range(LOOP_FROM):
                for k in range(4):
                    step(Plan(u, k))
            with eng.Fori(LOOP_FROM, LOOP_TO) as u:
                for k in range(4):
                    step(Plan(u, k))
            for u in range(LOOP_TO, STEPS_U):
                for k in range(4):
                    step(Plan(u, k))

        def ffn_run(eng, ffn):
            for t in range(RING):
                ffn(t, 0, t, [t - n >= 0 for n in range(4)])
            with eng.Fori(1, TILES // RING) as v:
                for i in range(RING):
                    ffn(v * RING + i, v, i, [True] * 4)
            for i in range(3):
                ffn(TILES + i, TILES // RING, i, [i - n < 0 for n in range(4)])

        block = stack.enter_context(nc.Block())

        @block.sync
        def _(sp):
            def load_in(g, par, used):
                sp.dma_start(x_in[:, par, :, :], x_t[g]).then_inc(s_in[par], 16)
                sp.dma_start(c_in[:, par, :, :], c_t[g]).then_inc(s_in[par], 16)

            load_in(0, 0, 0)
            for w, raw in ((Wq, raw_q), (Wk, raw_k), (Wv, raw_v)):
                sp.dma_start(raw, w).then_inc(s_raw, 16)
            sp.dma_start(raw_o.rearrange("p (m d) -> p m d", m=M8),
                         Wo.rearrange("(m p) d -> p m d", p=P)).then_inc(s_raw, 16)
            load_in(1, 1, 0)
            for g in (2, 3):
                sp.wait_ge(s_zm, 2 * (g - 1))
                load_in(g, g % 2, 1)
            sp.dma_start(w1_sb[:, :].rearrange("d (e f) -> d e f", e=E),
                         w1.rearrange("e d f -> d e f")).then_inc(s_ffn, 16)
            sp.dma_start(w2_sb[:, :].rearrange("p (e k d) -> p e k d", e=E, k=FK),
                         w2.rearrange("e (k p) d -> p e k d", p=P)).then_inc(s_ffn, 16)

            def step(p):
                if p.odd:
                    return
                ahead, now = p.group(-4), p.group(0)
                a = sp.snap(ahead) if ahead is not None and not p.fixed else ahead
                b = sp.snap(now) if now is not None and not p.fixed else now
                if ahead is not None:
                    sp.wait_ge(s_zm, 2 * (p.g + 3))
                    load_in(a, p.par(), 0)
                if now is not None:
                    if not (p.fixed and p.g < 2):
                        sp.wait_ge(s_x2, p.g - 1)
                    sp.dma_start(x_res[:, p.par(), :, :], x_t[b]).then_inc(s_res[p.par()], 16)

            run(sp, step)

            sp.wait_ge(s_cc, 3)
            sp.dma_start(rows_dram[E * REGION:E * REGION + P, :], pad_row[:, :]).then_inc(s_pad, 16)
            sp.wait_ge(s_qk, PAIRS)
            sp.dma_start(b1_sb, b1.rearrange("(a e) f -> a (e f)", a=1).to_broadcast([P, E * F])).then_inc(s_bias, 16)
            sp.dma_start(b2_sb, b2.rearrange("(a e) d -> a (e d)", a=1).to_broadcast([P, E * D])).then_inc(s_bias, 16)
            for i in range(2):
                sp.wait_ge(s_scat[i], 32 * (GROUPS // 2))
            sp.wait_ge(s_tab, 2)
            for e in range(E):
                start = sp.value_load(next_i[0:1, e:e + 1], min_val=e * REGION, max_val=e * REGION + TOK)
                sp.dma_start(rows_dram[bass.ds(start, P), :], pad_row[:, :]).then_inc(s_pad, 16)
            sp.wait_ge(s_pad, 16 * (E + 1))
            sp.wait_ge(s_pv, PAIRS)
            sp.wait_ge(s_tab, 13)

            def load_rows(t, i, trips):
                r = sp.value_load(row_tab[0:1, bass.ds(t, 1)], min_val=0, max_val=E * REGION)
                if not (isinstance(t, int) and t < RING):
                    sp.wait_ge(f_scat[i], 16 * trips)
                sp.dma_start(tile_rows[i], rows_dram[bass.ds(r, P), :]).then_inc(f_load[i], 16)

            for i in range(RING):
                load_rows(i, i, 0)
            with sp.Fori(1, TILES // RING) as v:
                for i in range(RING):
                    load_rows(v * RING + i, i, v)

        @block.gpsimd
        def _(pool):
            pool.memset(ident[:, :], 0.0).then_inc(s_const, 1)
            pool.memset(ones_b[:, :], 1.0).then_inc(s_const, 1)
            pool.memset(zero1[:, :], 0.0).then_inc(s_const, 1)
            pool.memset(pad_row[:, :], 0.0).then_inc(s_const, 1)
            pool.memset(one14[:, :], 1.0).then_inc(s_const, 1)
            pool.memset(mv[:, :, :], 1.0).then_inc(s_const, 1)
            pool.memset(var_mul[:, 0:2], 1.0 + EPS).then_inc(s_const, 1)
            pool.memset(var_mul[:, 2:6], 1.0).then_inc(s_const, 1)
            pool.memset(var_add[:, 0:2], EPS * EPS).then_inc(s_const, 1)
            pool.memset(var_add[:, 2:6], EPS).then_inc(s_const, 1)
            pool.iota(e_int[:, :, :], pattern=[[0, 2], [1, E]], base=0, channel_multiplier=0).then_inc(s_const, 1)
            pool.iota(r_int[:, :], pattern=[[REGION, E]], base=0, channel_multiplier=0).then_inc(s_const, 1)
            pool.iota(token[:, :], pattern=[[P, 2]], base=0, channel_multiplier=1).then_inc(s_const, 1)
            pool.iota(token_step[:, :], pattern=[[0, 2]], base=GT, channel_multiplier=0).then_inc(s_const, 1)
            pool.iota(t_int[:, :], pattern=[[1, TILES]], base=0, channel_multiplier=0).then_inc(s_const, 1)
            pool.wait_ge(s_const, 15)
            pool.affine_select(out=ident[:, :], in_=ident[:, :], compare_op=ALU.not_equal, fill=1.0, base=0,
                               pattern=[[-1, P]], channel_multiplier=1).then_inc(s_cc, 1)
            pool.affine_select(out=before[:, :], in_=ones_b[:, :], compare_op=ALU.is_gt, fill=0.0, base=0,
                               pattern=[[1, P]], channel_multiplier=-1).then_inc(s_cc, 1)
            pool.iota(pad_row[:, ROW - 1:ROW].bitcast(I32), pattern=[[0, 1]], base=TOK,
                      channel_multiplier=0).then_inc(s_cc, 1)

            def norm_in(p):
                g = p.group(-2)
                if g is None:
                    return
                par = p.par()
                r_x, r_c = (rstd[:, a:a + 2].unsqueeze(2) for a in (0, 2))
                sh_x, sh_c = (shift[:, a:a + 2].unsqueeze(2) for a in (0, 2))
                pool.wait_ge(s_newton, NEWT * (p.g + 3))
                if not (p.fixed and p.g < -1):
                    pool.wait_ge(s_prep, p.g + 2)
                pool.tensor_tensor(zx[:, :, :], x_in[:, par, :, :], r_x.to_broadcast([P, 2, D]),
                                   ALU.mult).then_inc(s_zm, 1)
                pool.tensor_tensor(zc[:, :, :], c_in[:, par, :, :], r_c.to_broadcast([P, 2, C]),
                                   ALU.mult).then_inc(s_zm, 1)
                pool.wait_ge(s_zm, 2 * (p.g + 3))
                pool.tensor_tensor(zx[:, :, :], zx[:, :, :], sh_x.to_broadcast([P, 2, D]), ALU.add).then_inc(s_z, 1)
                pool.tensor_tensor(zc[:, :, :], zc[:, :, :], sh_c.to_broadcast([P, 2, C]), ALU.add).then_inc(s_z, 1)

            def norm_x2(p):
                g = p.group(2)
                if g is None:
                    return
                par = p.par()
                n2 = rows[:, par, :, D:2 * D]
                pool.wait_ge(s_newton, NEWT * (p.g + 3))
                pool.tensor_tensor(n2, rows[:, par, :, 0:D], rstd[:, 4:6].unsqueeze(2).to_broadcast([P, 2, D]),
                                   ALU.mult).then_inc(s_n2m, 1)
                pool.wait_ge(s_n2m, p.g - 1)
                pool.tensor_tensor(n2, n2, shift[:, 4:6].unsqueeze(2).to_broadcast([P, 2, D]),
                                   ALU.add).then_inc(s_n2, 1)

            def split_in(p):
                g = p.group(-2)
                if g is None:
                    return
                par = p.par()
                pool.wait_ge(s_xf, 2 * (p.g + 3))
                if not (p.fixed and p.g < 0):
                    pool.wait_ge(s_job, 12 * (p.g + 1))
                pool.tensor_tensor(XT_h[:, par, :], xf[:, :], zero1[:, :].to_broadcast([P, GT]), ALU.add).then_inc(s_hi, 1)
                pool.tensor_tensor(CT_h[:, par, :], cf[:, :], zero1[0:C, :].to_broadcast([C, GT]), ALU.add).then_inc(s_hi, 1)
                pool.wait_ge(s_hi, 2 * (p.g + 3))
                pool.tensor_tensor(XT_l[:, par, :], xf[:, :], XT_h[:, par, :], ALU.subtract).then_inc(s_lo, 1)
                pool.tensor_tensor(CT_l[:, par, :], cf[:, :], CT_h[:, par, :], ALU.subtract).then_inc(s_lo, 1)

            def send(p):
                g = p.group(3)
                if g is None:
                    return
                par = p.par(3)
                pool.wait_ge(s_route, 6 * (p.g - 2))
                if not (p.fixed and p.g < 4):
                    pool.wait_ge(s_tok, p.g - 3)
                pool.tensor_tensor(rows[:, par, :, ROW - 1].bitcast(I32), token[:, :],
                                   zero1[:, :].bitcast(I32).to_broadcast([P, 2]), ALU.add).then_inc(s_id, 1)
                pool.wait_ge(s_place, 3 * (p.g - 2))
                pool.wait_ge(s_id, p.g - 2)
                pool.tensor_tensor(token[:, :], token[:, :], token_step[:, :], ALU.add).then_inc(s_tok, 1)
                for t in range(2):
                    pool.indirect_dma_start(rows_dram, bass.IndirectOffsetOnAxis(place_i[:, par, t:t + 1], 0),
                                            rows[:, par, t, :], None).then_inc(s_scat[par], 16)

            def step(p):
                if p.odd:
                    split_in(p)
                    send(p)
                else:
                    norm_in(p)
                    norm_x2(p)

            for g in (-2, -1):
                q = Plan(-1, 2 * (g + 2))
                norm_in(q)
                split_in(q)
            run(pool, step)

            def send_out(t, i, trips):
                pool.wait_ge(f_out, t + 1)
                pool.sem_inc(f_send, 1)
                pool.indirect_dma_start(out_rows, bass.IndirectOffsetOnAxis(tile_rows[i][:, ROW - 1:ROW].bitcast(I32), 0),
                                        tile_out[i], None, bounds_check=TOK - 1, oob_is_err=False).then_inc(f_scat[i], 16)

            with pool.Fori(0, TILES // RING) as v:
                for i in range(RING):
                    send_out(v * RING + i, i, v)
            for i in range(RING):
                pool.wait_ge(f_scat[i], 16 * (TILES // RING))

        @block.scalar
        def _(act):
            small = ((gx_col[:, :], g_x.rearrange("(p a) -> p a", a=1)), (bx_col[:, :], b_x.rearrange("(p a) -> p a", a=1)),
                     (gc_col[:, :], g_c.rearrange("(p a) -> p a", a=1)), (bc_col[:, :], b_c.rearrange("(p a) -> p a", a=1)),
                     (gates[:, 0:1], g_xattn.rearrange("(p a) -> p a", a=1).to_broadcast([P, 1])),
                     (gates[:, 1:2], g_ffn.rearrange("(p a) -> p a", a=1).to_broadcast([P, 1])),
                     (rw_sb[:, :], router_w))
            for dst, src in small:
                act.dma_start(dst, src).then_inc(s_small, 16)
            act.wait_ge(s_small, 16 * len(small))
            act.activation(tanhs[:, :], gates[:, :], ACT.Tanh).then_inc(s_tanh, 1)

            def weight_high(i, dst, raw):
                act.activation(dst, raw, ACT.Copy).then_inc(s_wh, 1)

            def prep(p):
                if p.group(-2) is None:
                    return
                act.wait_ge(s_prep, p.g + 3)
                if not (p.fixed and p.g < -1):
                    act.wait_ge(s_lo, 2 * (p.g + 2))
                act.activation(xf[:, :], psM[:, 0:GT], ACT.Identity, bias=bx_col[:, :], scale=gx_col[:, :]).then_inc(s_xf, 1)
                act.activation(cf[:, :], psM[0:C, GT:2 * GT], ACT.Identity, bias=bc_col[:, :], scale=gc_col[:, :]).then_inc(s_xf, 1)

            def job(p, n):
                if p.group(-1) is None:
                    return
                par = p.par(-1)
                act.wait_ge(s_job, 12 * (p.g + 1) + n + 1)
                if n < 4:
                    dst = QT[:, par, 2 * n:2 * n + 2, :].rearrange("p m t -> p (m t)")
                elif n == 4 or 7 <= n <= 9:
                    m = 0 if n == 4 else n - 6
                    dst = KT[:, par, 2 * m:2 * m + 2, :].rearrange("p m t -> p (m t)")
                else:
                    pr, half = (0, n - 5) if n < 7 else (1, n - 10)
                    dst = V[:, par, pr, 512 * half:512 * half + 512]
                act.activation(dst, psJ[n % 2][:, :], ACT.Copy).then_inc(s_jobev, 1)

            def values_high(p):
                s = p.pair(2)
                if s is None:
                    return
                act.wait_ge(s_pv, p.s - 1)
                dst = OT_h[:, :, (p.k % 2) * P:(p.k % 2 + 1) * P].rearrange("p m (b q) -> p b m q", b=2)
                act.activation(dst, psO[:, :].rearrange("p (b m q) -> p b m q", b=2, m=M8), ACT.Copy).then_inc(s_oh, 1)

            def probs_out(p, half):
                if p.pair(1) is None:
                    return
                act.wait_ge(s_pt, 2 * (p.s - 1) + half + 1)
                act.activation(PTs[:, half, :], psT[:, :], ACT.Copy).then_inc(s_ptev, 1)

            def expo(p):
                if p.pair(0) is None:
                    return
                act.wait_ge(s_sub, p.s + 1)
                act.activation(probs[:, p.k % 2, :, :], probs[:, p.k % 2, :, :], ACT.Exp, scale=SCALE).then_inc(s_exp, 1)

            def attn_out(p):
                if p.group(1) is None:
                    return
                act.wait_ge(s_oproj, p.g)
                act.activation(aT[:, :], psM[:, 0:GT], ACT.Copy, scale=tanhs[:, 0:1]).then_inc(s_aT, 1)

            def norm_T(p):
                if p.group(2) is None:
                    return
                act.wait_ge(s_postb, p.g - 1)
                act.activation(n2T[:, :], psM[:, 0:GT], ACT.Copy).then_inc(s_n2T, 1)

            def route_exp(p):
                if p.group(3) is None:
                    return
                act.wait_ge(s_dl, p.g - 2)
                act.activation(el[:, :, :], dl[:, :, :], ACT.Exp).then_inc(s_el, 1)

            def step(p):
                if p.odd:
                    job(p, 7)
                    job(p, 8)
                    job(p, 9)
                    expo(p)
                    norm_T(p)
                    values_high(p)
                    job(p, 10)
                    probs_out(p, 0)
                    prep(p)
                    job(p, 11)
                    probs_out(p, 1)
                    attn_out(p)
                else:
                    job(p, 0)
                    job(p, 1)
                    route_exp(p)
                    job(p, 2)
                    expo(p)
                    values_high(p)
                    job(p, 3)
                    probs_out(p, 0)
                    job(p, 4)
                    job(p, 5)
                    probs_out(p, 1)
                    job(p, 6)

            for i, (dst, raw) in enumerate(((Wq_h[:, :], raw_q), (Wk_h[:, :], raw_k), (Wv_h[:, :], raw_v),
                                            (Wo_h[:, :, :].rearrange("p m d -> p (m d)"), raw_o))):
                if i == 0:
                    act.wait_ge(s_raw, 64)
                weight_high(i, dst, raw)
            for g in (-2, -1):
                prep(Plan(-1, 2 * (g + 2)))
            for n in range(12):
                job(Plan(-1, 2), n)
            run(act, step)

            def ffn(t, v, i, on):
                if on[0]:
                    act.wait_ge(f_t1, t + 1)
                    act.activation(n2_T[i % 2], psJ[i % 2][:, 0:P], ACT.Copy).then_inc(f_t1ev, 1)
                if on[1]:
                    act.wait_ge(f_pre, t)
                    act.activation(hid[(i - 1) % 2], pre[(i - 1) % 2], ACT.Gelu).then_inc(f_gelu, 1)
                if on[2]:
                    act.wait_ge(f_t2, t - 1)
                    act.activation(hid_T[i % 2], psS[:, 512 * (i % 2):512 * (i % 2) + F], ACT.Copy).then_inc(f_t2ev, 1)

            ffn_run(act, ffn)

        @block.tensor
        def _(pe):
            misc = [None]

            def misc_free():
                if misc[0] is not None:
                    pe.wait_ge(*misc[0])

            def split3(outs, w_h, w_l, r_h, r_l):
                return [lambda: pe.matmul(outs, w_h, r_h, start=True, stop=False),
                        lambda: pe.matmul(outs, w_h, r_l, start=False, stop=False),
                        lambda: pe.matmul(outs, w_l, r_h, start=False, stop=True)]

            def prep(p):
                if p.group(-2) is None:
                    return
                misc_free()
                pe.wait_ge(s_z, 2 * (p.g + 3))
                for t in range(2):
                    pe.transpose(psM[:, P * t:P * t + P], zx[:, t, :], ident[:, :])
                for t in range(2):
                    last = pe.transpose(psM[0:C, GT + P * t:GT + P * t + P], zc[:, t, :], ident[:, :])
                last.then_inc(s_prep, 1)
                misc[0] = (s_xf, 2 * (p.g + 3))

            def job(p, n, half=None, ahead=None):
                if p.group(-1) is None:
                    if ahead:
                        ahead()
                    return
                par = p.par(-1)
                bank = psJ[n % 2]
                if half != 1:
                    if n == 0:
                        pe.wait_ge(s_lo, 2 * (p.g + 2))
                    if not (p.fixed and 12 * (p.g + 1) + n < 2):
                        pe.wait_ge(s_jobev, 12 * (p.g + 1) + n - 1)
                if n < 5 or 7 <= n <= 9:
                    w_h, w_l, r_h, r_l = (Wq_h, Wq_l, XT_h, XT_l) if n < 4 else (Wk_h, Wk_l, CT_h, CT_l)
                    m0 = 2 * n if n < 4 else 0 if n == 4 else 2 * (n - 6)
                    products = []
                    for i in range(2):
                        cols = slice((m0 + i) * P, (m0 + i + 1) * P)
                        products += split3(bank[:, GT * i:GT * i + GT], w_h[:, cols], w_l[:, cols], r_h[:, par, :], r_l[:, par, :])
                    middle = 3
                else:
                    pr, h = (0, n - 5) if n < 7 else (1, n - 10)
                    tok, cols = slice(pr * P, pr * P + P), slice(512 * h, 512 * h + 512)
                    products = split3(bank[:, :], CT_h[:, par, tok], CT_l[:, par, tok], Wv_h[:, cols], Wv_l[:, cols])
                    middle = 2
                products = {None: products, 0: products[:middle], 1: products[middle:]}[half]
                for product in products[:-1]:
                    product()
                if ahead:
                    ahead()
                last = products[-1]()
                if half != 0:
                    last.then_inc(s_job, 1)

            def scores(p, part_of_4):
                if p.pair(0) is None:
                    return
                tok = (p.k % 2) * P
                for g in range(HG // 4 * part_of_4, HG // 4 * (part_of_4 + 1)):
                    for b in range(2):
                        for c in range(2):
                            for r in range(2):
                                part = slice(64 * r, 64 * r + 64)
                                m = 2 * g + c
                                col = 512 * r + (2 * g + b) * SEQ
                                cols = slice(tok + SEQ * b, tok + SEQ * b + SEQ)
                                last = pe.matmul(psS[64 * c:64 * c + 64, col:col + SEQ],
                                                 QT[part, p.par(), m, cols], KT[part, p.par(), m, cols],
                                                 start=True, stop=True)
                if part_of_4 == 3:
                    last.then_inc(s_qk, 1)

            def value_sums(p, part_of_4):
                if p.pair(2) is None:
                    return
                for m in range(M8 // 4 * part_of_4, M8 // 4 * (part_of_4 + 1)):
                    for h in range(2):
                        for b in range(2):
                            part = slice(64 * b, 64 * b + 64)
                            head = 2 * m + h
                            col = 512 * b + m * SEQ
                            last = pe.matmul(psO[64 * h:64 * h + 64, col:col + SEQ],
                                             V[part, p.par(1), p.k % 2, head * DH:head * DH + DH],
                                             PTs[part, h, m * SEQ:(m + 1) * SEQ],
                                             start=True, stop=True)
                if part_of_4 == 3:
                    last.then_inc(s_pv, 1)

            def scores_ready(p):
                s = p.s + 1
                if p.fixed and s >= PAIRS:
                    return
                if not (p.fixed and s < 1):
                    pe.wait_ge(s_sub, s)
                if p.odd:
                    pe.wait_ge(s_jobev, 12 * (p.g + 1) + 10)

            def sums_ready(p):
                if p.pair(2) is None:
                    return
                pe.wait_ge(s_ptev, 2 * (p.s - 1))
                if not (p.fixed and p.s < 3):
                    pe.wait_ge(s_ol, p.s - 2)

            def probs_T(p, half):
                if p.pair(1) is None:
                    return
                if half == 0:
                    pe.wait_ge(s_norm, p.s)
                if not (p.fixed and 2 * (p.s - 1) + half < 1):
                    pe.wait_ge(s_ptev, 2 * (p.s - 1) + half)
                for g in range(HG):
                    src = probs[:, (p.k - 1) % 2, 8 * half + 2 * g:8 * half + 2 * g + 2, :].rearrange("p b k -> p (b k)")
                    last = pe.transpose(psT[:, P * g:P * g + P], src, ident[:, :])
                last.then_inc(s_pt, 1)

            def out_proj(p, ahead):
                if p.group(1) is None:
                    ahead()
                    return
                misc_free()
                pe.wait_ge(s_oh, 2 * p.g)
                for m in range(M8):
                    pe.matmul(psM[:, 0:GT], Wo_h[:, m, :], OT_h[:, m, :], start=(m == 0), stop=False)
                    pe.matmul(psM[:, 0:GT], Wo_l[:, m, :], OT_h[:, m, :], start=False, stop=False)
                pe.wait_ge(s_ol, 2 * p.g)
                for m in range(M8):
                    if m == M8 - 1:
                        ahead()
                    last = pe.matmul(psM[:, 0:GT], Wo_h[:, m, :], OT_l[:, m, :], start=False, stop=(m == M8 - 1))
                last.then_inc(s_oproj, 1)
                misc[0] = (s_aT, p.g)

            def post_a(p):
                if p.group(2) is None:
                    return
                misc_free()
                pe.wait_ge(s_aT, p.g - 1)
                for t in range(2):
                    last = pe.transpose(psM[:, P * t:P * t + P], aT[:, P * t:P * t + P], ident[:, :])
                last.then_inc(s_posta, 1)
                misc[0] = (s_x2, p.g - 1)

            def post_b(p):
                if p.group(2) is None:
                    return
                misc_free()
                pe.wait_ge(s_n2, p.g - 1)
                for t in range(2):
                    last = pe.transpose(psM[:, P * t:P * t + P], rows[:, p.par(), t, D:2 * D], ident[:, :])
                last.then_inc(s_postb, 1)
                misc[0] = (s_n2T, p.g - 1)

            def router(p):
                if p.group(3) is None:
                    return
                misc_free()
                pe.wait_ge(s_n2T, p.g - 2)
                for t in range(2):
                    last = pe.matmul(psM[:, E * t:E * t + E], n2T[:, P * t:P * t + P], rw_sb[:, :], start=True, stop=True)
                last.then_inc(s_logit, 1)
                misc[0] = (s_dl, p.g - 2)

            def rank(p):
                if p.group(3) is None:
                    return
                misc_free()
                pe.wait_ge(s_hot, p.g - 2)
                pe.matmul(psM[:, 0:E], before[:, :], onehot[:, 0, :], start=True, stop=True)
                pe.matmul(psM[:, E:2 * E], ones_b[:, :], onehot[:, 0, :], start=True, stop=False)
                pe.matmul(psM[:, E:2 * E], before[:, :], onehot[:, 1, :], start=False, stop=True)
                pe.matmul(psM[:, 2 * E:3 * E], ones_b[:, :], onehot[:, 0, :], start=True, stop=False)
                pe.matmul(psM[:, 2 * E:3 * E], ones_b[:, :], onehot[:, 1, :], start=False, stop=True).then_inc(s_rank, 1)
                misc[0] = (s_ranked, p.g - 2)

            def step(p):
                if p.k == 0:
                    misc[0] = (s_aT, p.g - 1) if p.group(2) is not None else misc[0]
                if p.odd:
                    scores(p, 0)
                    job(p, 7, 0)
                    scores(p, 1)
                    job(p, 7, 1)
                    scores(p, 2)
                    job(p, 8, 0)
                    scores(p, 3)
                    job(p, 8, 1, lambda: sums_ready(p))
                    value_sums(p, 0)
                    job(p, 9, 0)
                    value_sums(p, 1)
                    job(p, 9, 1)
                    value_sums(p, 2)
                    job(p, 10, 0)
                    post_b(p)
                    value_sums(p, 3)
                    job(p, 10, 1)
                    probs_T(p, 0)
                    job(p, 11, 0)
                    prep(p)
                    job(p, 11, 1)
                    probs_T(p, 1)
                    out_proj(p, lambda: scores_ready(p))
                else:
                    scores(p, 0)
                    job(p, 0, 0)
                    scores(p, 1)
                    job(p, 0, 1)
                    router(p)
                    scores(p, 2)
                    job(p, 1, 0)
                    scores(p, 3)
                    job(p, 1, 1, lambda: sums_ready(p))
                    value_sums(p, 0)
                    job(p, 2, 0)
                    post_a(p)
                    value_sums(p, 1)
                    job(p, 2, 1)
                    value_sums(p, 2)
                    job(p, 3, 0)
                    value_sums(p, 3)
                    job(p, 3, 1)
                    probs_T(p, 0)
                    job(p, 4)
                    job(p, 5, 0)
                    rank(p)
                    job(p, 5, 1)
                    probs_T(p, 1)
                    job(p, 6, ahead=lambda: scores_ready(p))

            pe.wait_ge(s_cc, 2)
            prep(Plan(-1, 0))
            prep(Plan(-1, 2))
            pe.wait_ge(s_wl, 4)
            for n in range(12):
                job(Plan(-1, 2), n)
            pe.wait_ge(s_jobev, 10)
            run(pe, step)

            def ffn(t, v, i, on):
                if on[0]:
                    if not (isinstance(t, int) and t < 2):
                        pe.wait_ge(f_t1ev, t - 1)
                    pe.wait_ge(f_load[i], 16 * (v + 1))
                    pe.transpose(psJ[i % 2][:, 0:P], tile_rows[i][:, D:2 * D], ident[:, :]).then_inc(f_t1, 1)
                if on[1]:
                    at = pe.value_load(f_tab[0:1, bass.ds(t - 1, 1)], min_val=0, max_val=(E - 1) * F)
                    bank = (psM, psT)[(i - 1) % 2]
                    pe.wait_ge(f_t1ev, t)
                    if not (isinstance(t, int) and t < 3):
                        pe.wait_ge(f_pre, t - 2)
                    pe.matmul(bank[:, 0:F], n2_T[(i - 1) % 2], w1_sb[:, bass.ds(at, F)], start=True, stop=True).then_inc(f_w1, 1)
                if on[2]:
                    pe.wait_ge(f_gelu, t - 1)
                    if not (isinstance(t, int) and t < 4):
                        pe.wait_ge(f_t2ev, t - 3)
                    for k in range(FK):
                        last = pe.transpose(psS[:, 512 * (i % 2) + P * k:512 * (i % 2) + P * k + P],
                                            hid[i % 2][:, P * k:P * k + P], ident[:, :])
                    last.then_inc(f_t2, 1)
                if on[3]:
                    at = pe.value_load(f_tab[0:1, bass.ds(t - 3, 1)], min_val=0, max_val=(E - 1) * F)
                    o = 512 * ((i - 3) % 2)
                    pe.wait_ge(f_t2ev, t - 2)
                    if not (isinstance(t, int) and t < 5):
                        pe.wait_ge(f_sum, t - 4)
                    for k in range(FK):
                        last = pe.matmul(psO[:, o:o + D], hid_T[(i - 1) % 2][:, P * k:P * k + P],
                                         w2_sb[:, bass.ds(at + k * D, D)], start=(k == 0), stop=(k == FK - 1))
                    last.then_inc(f_w2, 1)

            pe.wait_ge(s_ffn, 32)
            pe.wait_ge(s_tab, 13)
            ffn_run(pe, ffn)

        @block.vector
        def _(dve):
            def stats_in(p):
                if p.group(-2) is None:
                    return
                par = p.par()
                dve.wait_ge(s_in[par], 32 * p.uses(-2))
                if not (p.fixed and p.g < -1):
                    dve.wait_ge(s_agg, 4 * (p.g + 2))
                for t in range(2):
                    dve.bn_stats(bn6[:, t, :], x_in[:, par, t, :]).then_inc(s_stat, 1)
                for t in range(2):
                    dve.bn_stats(bn6[:, 2 + t, :], c_in[:, par, t, :]).then_inc(s_stat, 1)

            def stats_in_done(p):
                if p.group(-2) is not None:
                    dve.wait_ge(s_stat, 4 * (p.g + 3))
                    if not (p.fixed and p.g < -1):
                        dve.wait_ge(s_newton, NEWT * (p.g + 2))

            def means_in(p):
                if p.group(-2) is None:
                    return
                for t in range(4):
                    dve.bn_aggr(mv[:, t, :], bn6[:, t, :]).then_inc(s_agg, 1)

            def roots(p):
                if p.group(-2) is None and p.group(2) is None:
                    return
                n = NEWT * (p.g + 2)
                if p.group(-2) is not None:
                    dve.wait_ge(s_agg, 4 * (p.g + 3))
                if p.group(2) is not None:
                    dve.wait_ge(s_agg2, 2 * (p.g - 1))
                dve.tensor_tensor(nw[:, :], mv[:, :, 1], var_mul[:, :], ALU.mult).then_inc(s_newton, 1)
                dve.wait_ge(s_newton, n + 1)
                dve.tensor_tensor(nw[:, :], nw[:, :], var_add[:, :], ALU.add).then_inc(s_newton, 1)
                dve.wait_ge(s_newton, n + 2)
                if not (p.fixed and p.g < -1):
                    if not (p.fixed and p.g + 1 >= GROUPS):
                        dve.wait_ge(s_z, 2 * (p.g + 2))
                if not (p.fixed and not 0 <= p.g - 3 < GROUPS):
                    dve.wait_ge(s_n2, p.g - 2)
                dve.tensor_scalar(rstd[:, :].bitcast(I32), nw[:, :].bitcast(I32), -0.5, RSQRT_SEED,
                                  ALU.mult, ALU.add).then_inc(s_newton, 1)
                n += 3
                for _ in range(NEWTON):
                    dve.wait_ge(s_newton, n)
                    dve.tensor_tensor(nq[:, :], rstd[:, :], rstd[:, :], ALU.mult).then_inc(s_newton, 1)
                    dve.wait_ge(s_newton, n + 1)
                    dve.scalar_tensor_tensor(nq[:, :], nq[:, :], -0.5, nw[:, :], ALU.mult, ALU.mult).then_inc(s_newton, 1)
                    dve.wait_ge(s_newton, n + 2)
                    dve.scalar_tensor_tensor(rstd[:, :], nq[:, :], 1.5, rstd[:, :], ALU.add, ALU.mult).then_inc(s_newton, 1)
                    n += 3
                dve.wait_ge(s_newton, n)
                dve.scalar_tensor_tensor(shift[:, :], mv[:, :, 0], -1.0, rstd[:, :], ALU.mult, ALU.mult).then_inc(s_newton, 1)

            def scores_max(p):
                if p.pair(0) is None:
                    return
                dve.wait_ge(s_qk, p.s + 1)
                dve.tensor_reduce(row_max[:, :], psS[:, :].rearrange("p (n k) -> p n k", k=SEQ), AX.X,
                                  ALU.max).then_inc(s_max, 1)

            def scores_sub(p):
                if p.pair(0) is None:
                    return
                dve.wait_ge(s_max, p.s + 1)
                dve.tensor_tensor(probs[:, p.k % 2, :, :], psS[:, :].rearrange("p (n k) -> p n k", k=SEQ),
                                  row_max[:, :].unsqueeze(2).to_broadcast([P, 16, SEQ]), ALU.subtract).then_inc(s_sub, 1)

            def sums(p):
                if p.pair(0) is None:
                    return
                pr = probs[:, p.k % 2, :, :]
                dve.wait_ge(s_exp, p.s + 1)
                dve.tensor_reduce(row_sum[:, :], pr, AX.X, ALU.add).then_inc(s_sum, 1)
                dve.wait_ge(s_sum, p.s + 1)
                dve.reciprocal(row_inv[:, :], row_sum[:, :]).then_inc(s_inv, 1)

            def normalise(p):
                if p.pair(0) is None:
                    return
                pr = probs[:, p.k % 2, :, :]
                dve.wait_ge(s_inv, p.s + 1)
                dve.tensor_tensor(pr, pr, row_inv[:, :].unsqueeze(2).to_broadcast([P, 16, SEQ]), ALU.mult).then_inc(s_norm, 1)

            def values_low(p):
                if p.pair(2) is None:
                    return
                cols = slice((p.k % 2) * P, (p.k % 2 + 1) * P)
                hi = OT_h[:, :, cols].rearrange("p m (b q) -> p b m q", b=2)
                lo = OT_l[:, :, cols].rearrange("p m (b q) -> p b m q", b=2)
                dve.wait_ge(s_oh, p.s - 1)
                dve.tensor_tensor(lo, psO[:, :].rearrange("p (b m q) -> p b m q", b=2, m=M8), hi,
                                  ALU.subtract).then_inc(s_ol, 1)

            def residual(p):
                if p.group(2) is None:
                    return
                par = p.par()
                dve.wait_ge(s_res[par], 16 * p.uses(2))
                if not (p.fixed and p.g < 4):
                    dve.wait_ge(s_scat[par], 32 * p.uses(4))
                    dve.wait_ge(s_agg2, 2 * (p.g - 2))
                dve.wait_ge(s_posta, p.g - 1)
                dve.tensor_tensor(rows[:, par, :, 0:D], psM[:, 0:GT].rearrange("p (t d) -> p t d", t=2),
                                  x_res[:, par, :, :], ALU.add).then_inc(s_x2, 1)
                dve.wait_ge(s_x2, p.g - 1)
                for t in range(2):
                    dve.bn_stats(bn6[:, 4 + t, :], rows[:, par, t, 0:D]).then_inc(s_stat2, 1)

            def residual_done(p):
                if p.group(2) is not None:
                    dve.wait_ge(s_stat2, 2 * (p.g - 1))

            def means_x2(p):
                if p.group(2) is None:
                    return
                for t in range(2):
                    dve.bn_aggr(mv[:, 4 + t, :], bn6[:, 4 + t, :]).then_inc(s_agg2, 1)

            def route(p):
                if p.group(3) is None:
                    return
                n, par = 6 * (p.g - 3), p.par(3)
                logits = psM[:, 0:2 * E].rearrange("p (t e) -> p t e", t=2)
                dve.wait_ge(s_logit, p.g - 2)
                dve.tensor_reduce(lmax[:, :], logits, AX.X, ALU.max).then_inc(s_lmax, 1)
                dve.wait_ge(s_lmax, p.g - 2)
                dve.tensor_tensor(dl[:, :, :], logits, lmax[:, :].unsqueeze(2).to_broadcast([P, 2, E]),
                                  ALU.subtract).then_inc(s_dl, 1)
                dve.wait_ge(s_dl, p.g - 2)
                dve.tensor_scalar(cand[:, :, :], dl[:, :, :], 0.0, 2.0 * E, ALU.is_lt, ALU.mult).then_inc(s_route, 1)
                dve.wait_ge(s_route, n + 1)
                dve.tensor_tensor(cand[:, :, :], cand[:, :, :], e_iota[:, :, :], ALU.add).then_inc(s_route, 1)
                dve.wait_ge(s_route, n + 2)
                dve.tensor_reduce(first[:, :], cand[:, :, :], AX.X, ALU.min).then_inc(s_route, 1)
                dve.wait_ge(s_route, n + 3)
                dve.tensor_tensor(onehot[:, :, :], e_iota[:, :, :], first[:, :].unsqueeze(2).to_broadcast([P, 2, E]),
                                  ALU.is_equal).then_inc(s_hot, 1)

            def weight(p):
                if p.group(3) is None:
                    return
                n, par = 6 * (p.g - 3), p.par(3)
                dve.wait_ge(s_el, p.g - 2)
                dve.tensor_reduce(den[:, :], el[:, :, :], AX.X, ALU.add).then_inc(s_route, 1)
                dve.wait_ge(s_route, n + 4)
                dve.reciprocal(inv[:, :], den[:, :]).then_inc(s_route, 1)
                dve.wait_ge(s_route, n + 5)
                dve.tensor_scalar(rows[:, par, :, 2 * D], inv[:, :], tanhs[:, 1:2], None, ALU.mult).then_inc(s_route, 1)

            def places(p):
                if p.group(3) is None:
                    return
                n, par = 3 * (p.g - 3), p.par(3)
                dve.wait_ge(s_rank, p.g - 2)
                if not (p.fixed and p.g < 4):
                    dve.wait_ge(s_ranked, p.g - 3)
                dve.tensor_tensor(place[:, :, :], psM[:, 0:2 * E].rearrange("p (t e) -> p t e", t=2),
                                  next_row[:, :].unsqueeze(1).to_broadcast([P, 2, E]), ALU.add).then_inc(s_place, 1)
                dve.wait_ge(s_place, n + 1)
                dve.tensor_tensor(next_row[:, :], next_row[:, :], psM[:, 2 * E:3 * E], ALU.add).then_inc(s_ranked, 1)
                dve.tensor_tensor(place[:, :, :], place[:, :, :], onehot[:, :, :], ALU.mult).then_inc(s_place, 1)
                dve.wait_ge(s_place, n + 2)
                with nc.allow_low_precision(reason="whole numbers below 2**24"):
                    dve.tensor_reduce(place_i[:, par, :], place[:, :, :], AX.X, ALU.add).then_inc(s_place, 1)

            def step(p):
                if p.odd:
                    scores_max(p)
                    scores_sub(p)
                    sums(p)
                    values_low(p)
                    normalise(p)
                else:
                    stats_in(p)
                    route(p)
                    scores_max(p)
                    stats_in_done(p)
                    scores_sub(p)
                    means_in(p)
                    residual(p)
                    residual_done(p)
                    sums(p)
                    means_x2(p)
                    values_low(p)
                    normalise(p)
                    places(p)
                    weight(p)
                    roots(p)

            dve.wait_ge(s_const, 15)
            dve.tensor_copy(e_iota[:, :, :], e_int[:, :, :])
            dve.tensor_copy(next_row[:, :], r_int[:, :])
            dve.tensor_copy(t_f[:, :], t_int[:, :]).then_inc(s_tab, 1)
            for g in (-2, -1):
                q = Plan(-1, 2 * (g + 2))
                stats_in(q)
                stats_in_done(q)
                means_in(q)
                roots(q)
                if g == -2:
                    for i, (lo, hi, raw) in enumerate(((Wq_l[:, :], Wq_h[:, :], raw_q), (Wk_l[:, :], Wk_h[:, :], raw_k),
                                                       (Wv_l[:, :], Wv_h[:, :], raw_v),
                                                       (Wo_l[:, :, :].rearrange("p m d -> p (m d)"),
                                                        Wo_h[:, :, :].rearrange("p m d -> p (m d)"), raw_o))):
                        dve.wait_ge(s_wh, i + 1)
                        dve.tensor_tensor(lo, raw, hi, ALU.subtract).then_inc(s_wl, 1)
            dve.wait_ge(s_tanh, 1)
            dve.wait_ge(s_tab, 1)
            run(dve, step)

            def link(ins, n):
                ins.then_inc(s_tab, 1)
                dve.wait_ge(s_tab, n)

            dve.wait_ge(s_ranked, GROUPS)
            link(dve.tensor_copy(next_i[:, :], next_row[0:1, :]), 2)
            link(dve.tensor_tensor(n_tiles[:, :], next_row[0:1, :], r_int[0:1, :], ALU.subtract), 3)
            link(dve.tensor_scalar(ends_i[:, :], n_tiles[:, :], float(P - 1), None, ALU.add), 4)
            link(dve.tensor_scalar(ends_i[:, :], ends_i[:, :], 7, None, ALU.logical_shift_right), 5)
            link(dve.tensor_copy(n_tiles[:, :], ends_i[:, :]), 6)
            link(dve.tensor_tensor_scan(cum[:, :], one14[:, :], n_tiles[:, :], 0.0, ALU.mult, ALU.add), 7)
            link(dve.tensor_tensor(past[:, :, :], t_f[:, :].unsqueeze(2).to_broadcast([1, TILES, E]),
                                   cum[:, :].unsqueeze(1).to_broadcast([1, TILES, E]), ALU.is_ge), 8)
            link(dve.tensor_reduce(t_expert[:, :], past[:, :, :], AX.X, ALU.add), 9)
            link(dve.tensor_tensor(past[:, :, :], past[:, :, :], n_tiles[:, :].unsqueeze(1).to_broadcast([1, TILES, E]),
                                   ALU.mult), 10)
            link(dve.tensor_reduce(t_start[:, :], past[:, :, :], AX.X, ALU.add), 11)
            link(dve.tensor_tensor(t_row[:, :], t_f[:, :], t_start[:, :], ALU.subtract), 12)
            dve.tensor_scalar(f_tab[:, :], t_expert[:, :], float(E - 1), float(F), ALU.min, ALU.mult)
            dve.tensor_scalar(d_tab[:, :], t_expert[:, :], float(E - 1), float(D), ALU.min, ALU.mult)
            dve.tensor_scalar(t_start[:, :], t_expert[:, :], float(REGION), None, ALU.mult).then_inc(s_dummy, 1)
            dve.wait_ge(s_dummy, 1)
            dve.scalar_tensor_tensor(t_row[:, :], t_row[:, :], float(P), t_start[:, :], ALU.mult, ALU.add).then_inc(s_dummy, 1)
            dve.wait_ge(s_dummy, 2)
            dve.tensor_scalar(row_tab[:, :], t_row[:, :], float(E * REGION), None, ALU.min).then_inc(s_tab, 1)

            def ffn(t, v, i, on):
                if on[1]:
                    at = dve.value_load(f_tab[0:1, bass.ds(t - 1, 1)], min_val=0, max_val=(E - 1) * F)
                    if not (isinstance(t, int) and t < 3):
                        dve.wait_ge(f_gelu, t - 2)
                    dve.wait_ge(f_w1, t)
                    dve.tensor_tensor(pre[(i - 1) % 2], (psM, psT)[(i - 1) % 2][:, 0:F], b1_sb[:, bass.ds(at, F)],
                                      ALU.add).then_inc(f_pre, 1)
                if on[3]:
                    r = (i - 3) % RING
                    o = 512 * ((i - 3) % 2)
                    at = dve.value_load(d_tab[0:1, bass.ds(t - 3, 1)], min_val=0, max_val=(E - 1) * D)
                    if not (isinstance(t, int) and t < 4):
                        dve.wait_ge(f_out, t - 3)
                    dve.wait_ge(f_w2, t - 2)
                    dve.tensor_tensor(ysum[:, :], psO[:, o:o + D], b2_sb[:, bass.ds(at, D)], ALU.add).then_inc(f_sum, 1)
                    if not (isinstance(t, int) and t - 3 < RING):
                        dve.wait_ge(f_scat[r], 16 * (v + (i - 3) // RING))
                    dve.wait_ge(f_sum, t - 2)
                    dve.scalar_tensor_tensor(tile_out[r], ysum[:, :], tile_rows[r][:, 2 * D:2 * D + 1],
                                             tile_rows[r][:, 0:D], ALU.mult, ALU.add).then_inc(f_out, 1)

            dve.wait_ge(s_bias, 32)
            dve.wait_ge(s_tab, 13)
            ffn_run(dve, ffn)


_INS = ['x', 'ctx_768', 'g_xattn', 'g_ffn', 'L0_xattn_g_x', 'L0_xattn_b_x', 'L0_xattn_g_c', 'L0_xattn_b_c',
        'L0_xattn_Wq', 'L0_xattn_Wk', 'L0_xattn_Wv', 'L0_xattn_Wo', 'L0_ffn_router_w', 'L0_ffn_w1', 'L0_ffn_b1',
        'L0_ffn_w2', 'L0_ffn_b2']


def kernel(**inputs):
    import numpy as _np
    import concourse.bacc as _bacc
    from concourse import mybir as _mybir
    from concourse.bass_utils import run_bass_kernel_spmd as _run

    nc = _bacc.Bacc("TRN2", target_bir_lowering=False, num_devices=1)
    arrays, args = {}, []
    for name in _INS:
        a = _np.ascontiguousarray(inputs[name])
        arrays[f"in_{name}_dram"] = a
        args.append(nc.dram_tensor(f"in_{name}_dram", a.shape, _mybir.dt.from_np(a.dtype), kind="ExternalInput").ap())
    shape = tuple(inputs['x'].shape)
    args.append(nc.dram_tensor("out_dram", shape, _mybir.dt.from_np(_np.dtype('float32')), kind="ExternalOutput").ap())
    gated_block_kernel(nc, *args)
    r = _run(nc, [arrays], core_ids=[0])
    return r.results[0]["out_dram"]
```

```python
from contextlib import ExitStack

import concourse.bass as bass
from concourse import mybir

F32 = mybir.dt.float32
F32R = mybir.dt.float32r
BF16 = mybir.dt.bfloat16
I32 = mybir.dt.int32
ALU = mybir.AluOpType
ACT = mybir.ActivationFunctionType
AX = mybir.AxisListType

P = 128
SEQ = 64
DH = 64
EPS = 1e-5
SCALE = float(DH) ** -0.5
RSQRT_SEED = float(0x5F3759DF)
NEWTON = 3
LOOP_FROM, LOOP_TO = 2, 14
RING = 8


def gated_block_kernel(nc, x, ctx768, g_xattn, g_ffn, g_x, b_x, g_c, b_c, Wq, Wk, Wv, Wo,
                       router_w, w1, b1, w2, b2, out):
    B, N, D = x.shape
    C = ctx768.shape[2]
    INNER = Wq.shape[1]
    H = INNER // DH
    M8 = INNER // P
    HG = H // 4
    E, _, F = w1.shape
    FK = F // P
    TOK = B * N
    GT = 2 * P
    GROUPS = TOK // GT
    PAIRS = TOK // P
    REGION = P + TOK
    ROW = D + D + 2
    TILES = -(-(TOK // P + E - 1) // RING) * RING
    assert N == SEQ and D == P and GROUPS == 2 * (LOOP_TO + 2)

    rows_dram = nc.dram_tensor("rows_by_expert", [E * REGION + P, ROW], F32, kind="Internal").ap()

    x_t = x.rearrange("b n d -> (b n) d").rearrange("(g j p) d -> g p j d", j=2, p=P)
    c_t = ctx768.rearrange("b n d -> (b n) d").rearrange("(g j p) d -> g p j d", j=2, p=P)
    out_rows = out.rearrange("b n d -> (b n) d")

    with ExitStack() as stack:
        def sb(name, shape, dt=F32):
            return stack.enter_context(nc.sbuf_tensor(name, shape, dt))

        def psum(name, shape):
            return stack.enter_context(nc.psum_tensor(name, shape, F32))

        def sem(name):
            return stack.enter_context(nc.semaphore(name))

        Wq_h, Wq_l = sb("Wq_h", [P, INNER], F32R), sb("Wq_l", [P, INNER], F32R)
        Wk_h, Wk_l = sb("Wk_h", [C, INNER], F32R), sb("Wk_l", [C, INNER], F32R)
        Wv_h, Wv_l = sb("Wv_h", [C, INNER], F32R), sb("Wv_l", [C, INNER], F32R)
        Wo_h, Wo_l = sb("Wo_h", [P, M8, D], F32R), sb("Wo_l", [P, M8, D], F32R)
        w1_sb = sb("w1_sb", [P, E * F])
        w2_sb = sb("w2_sb", [P, E * F])
        rw_sb = sb("rw_sb", [P, E])
        gx_col, bx_col = sb("gx_col", [P, 1]), sb("bx_col", [P, 1])
        gc_col, bc_col = sb("gc_col", [C, 1]), sb("bc_col", [C, 1])
        gates = sb("gates", [P, 2])
        tanhs = sb("tanhs", [P, 2])
        ident = sb("ident", [P, P])
        before = sb("before", [P, P], BF16)
        ones_b = sb("ones_b", [P, P], BF16)
        zero1 = sb("zero1", [P, 1])
        var_mul, var_add = sb("var_mul", [P, 6]), sb("var_add", [P, 6])
        e_int, e_iota = sb("e_int", [P, 2, E], I32), sb("e_iota", [P, 2, E])
        r_int = sb("r_int", [P, E], I32)
        token = sb("token", [P, 2], I32)
        token_step = sb("token_step", [P, 2], I32)
        x_in, c_in = sb("x_in", [P, 2, 2, D]), sb("c_in", [P, 2, 2, C])
        x_res = sb("x_res", [P, 2, 2, D])
        zx, zc = sb("zx", [P, 2, D]), sb("zc", [P, 2, C])
        xf, cf = sb("xf", [P, GT]), sb("cf", [C, GT])
        XT_h, XT_l = sb("XT_h", [P, 2, GT], F32R), sb("XT_l", [P, 2, GT], F32R)
        CT_h, CT_l = sb("CT_h", [C, 2, GT], F32R), sb("CT_l", [C, 2, GT], F32R)
        QT, KT = sb("QT", [P, 2, M8, GT]), sb("KT", [P, 2, M8, GT])
        V = sb("V", [P, 2, 2, INNER])
        probs = sb("probs", [P, 2, 2 * HG * 2, SEQ])
        row_max, row_sum, row_inv = sb("row_max", [P, 16]), sb("row_sum", [P, 16]), sb("row_inv", [P, 16])
        PTs = sb("PTs", [P, 2, 4 * P])
        OT_h, OT_l = sb("OT_h", [P, M8, GT], F32R), sb("OT_l", [P, M8, GT], F32R)
        aT = sb("aT", [P, GT])
        rows = sb("rows", [P, 2, 2, ROW])
        n2T = sb("n2T", [P, GT])
        bn6 = sb("bn6", [P, 6, 6])
        mv = sb("mv", [P, 6, 2])
        nw, nq = sb("nw", [P, 6]), sb("nq", [P, 6])
        rstd, shift = sb("rstd", [P, 6]), sb("shift", [P, 6])
        lmax = sb("lmax", [P, 2])
        dl, el, cand = sb("dl", [P, 2, E]), sb("el", [P, 2, E]), sb("cand", [P, 2, E])
        first, den, inv = sb("first", [P, 2]), sb("den", [P, 2]), sb("inv", [P, 2])
        onehot = sb("onehot", [P, 2, E], BF16)
        place = sb("place", [P, 2, E])
        place_i = sb("place_i", [P, 2, 2], I32)
        next_row = sb("next_row", [P, E])
        pad_row = sb("pad_row", [P, ROW])
        ends_i = sb("ends_i", [P, E], I32)
        n_tiles, cum, one14 = sb("n_tiles", [P, E]), sb("cum", [P, E]), sb("one14", [P, E])
        move = sb("move", [P, E])
        past, past_move = sb("past", [P, E]), sb("past_move", [P, E])
        t_int, t_f = sb("t_int", [P, 2], I32), sb("t_f", [P, 2])
        t_expert, t_row, t_base = sb("t_expert", [P, 1]), sb("t_row", [P, 1]), sb("t_base", [P, 1])
        t_cols = sb("t_cols", [P, 4])
        table = sb("table", [1, 4, P], I32)
        row_tab, f_tab, d_tab, k_tab = (table[:, i, :] for i in range(4))
        b1_rows = sb("b1_rows", [E * FK, P])
        b1_sb = sb("b1_sb", [P, E * FK])
        b2_sb = sb("b2_sb", [P, E * D])
        gelu_warm = sb("gelu_warm", [P, 1])
        tile_token = sb("tile_token", [P, RING], I32)

        QTf = QT[:, :, :, :].rearrange("p a m t -> p (a m t)")
        KTf = KT[:, :, :, :].rearrange("p a m t -> p (a m t)")
        Vf = V[:, :, :, :].rearrange("p a m t -> p (a m t)")
        HALF = M8 * GT
        raw_q, raw_k = QTf[:, HALF:HALF + INNER], QTf[0:C, HALF + INNER:HALF + 2 * INNER]
        raw_v, raw_o = KTf[0:C, HALF:HALF + INNER], KTf[:, HALF + INNER:HALF + 2 * INNER]
        n2_T = [KTf[:, P * i:P * (i + 1)] for i in range(2)]
        hid_T = [KTf[:, 2 * P + F * i:2 * P + F * (i + 1)] for i in range(2)]
        w1_tile = [KTf[:, 2 * P + F * i:2 * P + F * (i + 1)] for i in range(2, 4)]
        tile_rows = [Vf[:, ROW * i:ROW * (i + 1)] for i in range(RING)]
        at = RING * ROW
        tile_out = [Vf[:, at + D * i:at + D * (i + 1)] for i in range(RING)]
        ysum = sb("ysum", [P, D])

        psJ = [psum("psJ0", [P, 512]), psum("psJ1", [P, 512])]
        psM = psum("psM", [P, 512])
        psT = psum("psT", [P, 512])
        psS = psum("psS", [P, 1024])
        psO = psum("psO", [P, 1024])

        s_small, s_raw, s_ffn, s_bias = sem("s_small"), sem("s_raw"), sem("s_ffn"), sem("s_bias")
        s_in = [sem("s_in0"), sem("s_in1")]
        s_res = [sem("s_res0"), sem("s_res1")]
        s_const, s_cc, s_tanh = sem("s_const"), sem("s_cc"), sem("s_tanh")
        s_wh, s_wl = sem("s_wh"), sem("s_wl")
        s_stat = sem("s_stat")
        s_agg = sem("s_agg")
        s_stat2, s_agg2 = sem("s_stat2"), sem("s_agg2")
        s_newton = sem("s_newton")
        s_zm, s_z = sem("s_zm"), sem("s_z")
        s_prep, s_xf = sem("s_prep"), sem("s_xf")
        s_hi, s_lo = sem("s_hi"), sem("s_lo")
        s_job, s_jobev = sem("s_job"), sem("s_jobev")
        s_qk, s_max, s_sub, s_exp = sem("s_qk"), sem("s_max"), sem("s_sub"), sem("s_exp")
        s_sum, s_inv, s_norm = sem("s_sum"), sem("s_inv"), sem("s_norm")
        s_pt, s_ptev = sem("s_pt"), sem("s_ptev")
        s_pv, s_oh, s_ol = sem("s_pv"), sem("s_oh"), sem("s_ol")
        s_oproj, s_aT = sem("s_oproj"), sem("s_aT")
        s_posta, s_x2 = sem("s_posta"), sem("s_x2")
        s_n2m, s_n2 = sem("s_n2m"), sem("s_n2")
        s_postb, s_n2T = sem("s_postb"), sem("s_n2T")
        s_logit, s_lmax, s_dl, s_el = sem("s_logit"), sem("s_lmax"), sem("s_dl"), sem("s_el")
        s_route = sem("s_route")
        s_hot = sem("s_hot")
        s_rank, s_ranked = sem("s_rank"), sem("s_ranked")
        s_place = sem("s_place")
        s_id, s_tok = sem("s_id"), sem("s_tok")
        s_scat = [sem("s_scat0"), sem("s_scat1")]
        s_pad, s_link = sem("s_pad"), sem("s_link")
        s_cols, s_tabT, s_tab = sem("s_cols"), sem("s_tabT"), sem("s_tab")
        s_b1T, s_b1 = sem("s_b1T"), sem("s_b1")
        f_load = [sem(f"f_load{i}") for i in range(RING)]
        f_scat = [sem(f"f_scat{i}") for i in range(RING)]
        f_t1, f_t1ev, f_w1, f_gelu = sem("f_t1"), sem("f_t1ev"), sem("f_w1"), sem("f_gelu")
        f_pick = sem("f_pick")
        f_w2, f_sum, f_out = sem("f_w2"), sem("f_sum"), sem("f_out")
        f_send = sem("f_send")

        NEWT = 3 + 3 * NEWTON + 1
        N_SMALL = 10 * 16

        class Plan:

            def __init__(self, u, k, tail=False):
                self.k, self.j = k, k // 2
                self.odd = k % 2 == 1
                self.g = 2 * u + k // 2
                self.s = 4 * u + k
                self.u = u
                self.fixed = isinstance(u, int)

            def group(self, lag):
                g = self.g - lag
                if self.fixed and not 0 <= g < GROUPS:
                    return None
                return g

            def pair(self, lag):
                s = self.s - lag
                if self.fixed and not 0 <= s < PAIRS:
                    return None
                return s

            def par(self, lag=0):
                return (self.j - lag) % 2

            def uses(self, lag):
                return self.u + (self.j - lag - self.par(lag)) // 2 + 1

        STEPS_U = GROUPS // 2 + 2

        def run(eng, step):
            for u in range(LOOP_FROM):
                for k in range(4):
                    step(Plan(u, k))
            with eng.Fori(LOOP_FROM, LOOP_TO) as u:
                for k in range(4):
                    step(Plan(u, k))
            for u in range(LOOP_TO, STEPS_U):
                for k in range(4):
                    step(Plan(u, k))

        BACK = 4

        def entries(engine, tab, v, first, end, most):
            at = v * RING + first
            _, values = nc.values_load_multi_w_load_instructions(
                tab[0:1, bass.ds(at, end - first)], engines=[engine], min_val=0, max_val=most)
            return values

        def ffn_run(eng, engine, tab, most, ffn):
            e = entries(engine, tab, 0, 0, RING, most)
            for t in range(RING):
                ffn(t, 0, t, [t - n >= 0 for n in range(3)], [e[t - n] if t >= n else None for n in range(3)])
            with eng.Fori(1, TILES // RING) as v:
                e = entries(engine, tab, v, -BACK, RING, most)
                for i in range(RING):
                    ffn(v * RING + i, v, i, [True] * 3, [e[BACK + i - n] for n in range(3)])
            e = entries(engine, tab, TILES // RING, -BACK, 0, most)
            for i in range(2):
                ffn(TILES + i, TILES // RING, i, [i - n < 0 for n in range(3)],
                    [e[BACK + i - n] if i < n else None for n in range(3)])

        block = stack.enter_context(nc.Block())

        @block.sync
        def _(sp):
            def load_in(g, par, used):
                sp.dma_start(x_in[:, par, :, :], x_t[g]).then_inc(s_in[par], 16)
                sp.dma_start(c_in[:, par, :, :], c_t[g]).then_inc(s_in[par], 16)

            load_in(0, 0, 0)
            for w, raw in ((Wq, raw_q), (Wk, raw_k), (Wv, raw_v)):
                sp.dma_start(raw, w).then_inc(s_raw, 16)
            sp.dma_start(raw_o.rearrange("p (m d) -> p m d", m=M8),
                         Wo.rearrange("(m p) d -> p m d", p=P)).then_inc(s_raw, 16)
            load_in(1, 1, 0)
            for g in (2, 3):
                sp.wait_ge(s_zm, 2 * (g - 1))
                load_in(g, g % 2, 1)
            sp.dma_start(w1_sb[:, :].rearrange("d (e f) -> d e f", e=E),
                         w1.rearrange("e d f -> d e f")).then_inc(s_ffn, 16)
            sp.dma_start(w2_sb[:, :].rearrange("p (e k d) -> p e k d", e=E, k=FK),
                         w2.rearrange("e (k p) d -> p e k d", p=P)).then_inc(s_ffn, 16)
            sp.dma_start(b1_rows[:, :], b1.rearrange("e (k p) -> (e k) p", p=P)).then_inc(s_bias, 16)
            sp.dma_start(b2_sb[:, :], b2.rearrange("(a e) d -> a (e d)", a=1).to_broadcast([P, E * D])).then_inc(s_bias, 16)
            sp.wait_ge(s_cc, 3)
            sp.dma_start(rows_dram[0:E * REGION, :].rearrange("(e r) c -> r e c", e=E)[0:P],
                         pad_row[:, :].unsqueeze(1).to_broadcast([P, E, ROW])).then_inc(s_pad, 16)
            sp.dma_start(rows_dram[E * REGION:E * REGION + P, :], pad_row[:, :]).then_inc(s_pad, 16)

            def step(p):
                if p.odd:
                    return
                ahead, now = p.group(-4), p.group(0)
                a = sp.snap(ahead) if ahead is not None and not p.fixed else ahead
                b = sp.snap(now) if now is not None and not p.fixed else now
                if ahead is not None:
                    sp.wait_ge(s_zm, 2 * (p.g + 3))
                    load_in(a, p.par(), 0)
                if now is not None:
                    if not (p.fixed and p.g < 2):
                        sp.wait_ge(s_x2, p.g - 1)
                    sp.dma_start(x_res[:, p.par(), :, :], x_t[b]).then_inc(s_res[p.par()], 16)

            run(sp, step)

            for i in range(2):
                sp.wait_ge(s_scat[i], 32 * (GROUPS // 2))
            sp.wait_ge(s_pad, 32)
            sp.wait_ge(s_pv, PAIRS)
            sp.wait_ge(s_tab, 1)

            def load_rows(t, r, i, trips):
                if not (isinstance(t, int) and t < RING):
                    sp.wait_ge(f_out, t - RING + 1)
                sp.dma_start(tile_rows[i], rows_dram[bass.ds(r, P), :]).then_inc(f_load[i], 16)

            starts = entries(mybir.EngineType.SP, row_tab, 0, 0, RING, E * REGION)
            for i in range(RING):
                load_rows(i, starts[i], i, 0)
            with sp.Fori(1, TILES // RING) as v:
                starts = entries(mybir.EngineType.SP, row_tab, v, 0, RING, E * REGION)
                for i in range(RING):
                    load_rows(v * RING + i, starts[i], i, v)

        @block.gpsimd
        def _(pool):
            pool.memset(ident[:, :], 0.0).then_inc(s_const, 1)
            pool.memset(ones_b[:, :], 1.0).then_inc(s_const, 1)
            pool.memset(zero1[:, :], 0.0).then_inc(s_const, 1)
            pool.memset(pad_row[:, :], 0.0).then_inc(s_const, 1)
            pool.memset(one14[:, :], 1.0).then_inc(s_const, 1)
            pool.memset(mv[:, :, :], 1.0).then_inc(s_const, 1)
            pool.memset(var_mul[:, 0:2], 1.0 + EPS).then_inc(s_const, 1)
            pool.memset(var_mul[:, 2:6], 1.0).then_inc(s_const, 1)
            pool.memset(var_add[:, 0:2], EPS * EPS).then_inc(s_const, 1)
            pool.memset(var_add[:, 2:6], EPS).then_inc(s_const, 1)
            pool.iota(e_int[:, :, :], pattern=[[0, 2], [1, E]], base=0, channel_multiplier=0).then_inc(s_const, 1)
            pool.iota(r_int[:, :], pattern=[[REGION, E]], base=P, channel_multiplier=0).then_inc(s_const, 1)
            pool.iota(token[:, :], pattern=[[P, 2]], base=0, channel_multiplier=1).then_inc(s_const, 1)
            pool.iota(token_step[:, :], pattern=[[0, 2]], base=GT, channel_multiplier=0).then_inc(s_const, 1)
            pool.iota(t_int[:, 0:1], pattern=[[0, 1]], base=0, channel_multiplier=1).then_inc(s_const, 1)
            pool.iota(t_int[:, 1:2], pattern=[[0, 1]], base=-P, channel_multiplier=-P).then_inc(s_const, 1)
            pool.memset(move[:, :], 2.0 * E * REGION).then_inc(s_const, 1)
            pool.wait_ge(s_const, 17)
            pool.affine_select(out=ident[:, :], in_=ident[:, :], compare_op=ALU.not_equal, fill=1.0, base=0,
                               pattern=[[-1, P]], channel_multiplier=1).then_inc(s_cc, 1)
            pool.affine_select(out=before[:, :], in_=ones_b[:, :], compare_op=ALU.is_gt, fill=0.0, base=0,
                               pattern=[[1, P]], channel_multiplier=-1).then_inc(s_cc, 1)
            pool.iota(pad_row[:, ROW - 1:ROW].bitcast(I32), pattern=[[0, 1]], base=TOK,
                      channel_multiplier=0).then_inc(s_cc, 1)

            def norm_in(p):
                g = p.group(-2)
                if g is None:
                    return
                par = p.par()
                r_x, r_c = (rstd[:, a:a + 2].unsqueeze(2) for a in (0, 2))
                sh_x, sh_c = (shift[:, a:a + 2].unsqueeze(2) for a in (0, 2))
                pool.wait_ge(s_newton, NEWT * (p.g + 3))
                if not (p.fixed and p.g < -1):
                    pool.wait_ge(s_prep, p.g + 2)
                pool.tensor_tensor(zx[:, :, :], x_in[:, par, :, :], r_x.to_broadcast([P, 2, D]),
                                   ALU.mult).then_inc(s_zm, 1)
                pool.tensor_tensor(zc[:, :, :], c_in[:, par, :, :], r_c.to_broadcast([P, 2, C]),
                                   ALU.mult).then_inc(s_zm, 1)
                pool.wait_ge(s_zm, 2 * (p.g + 3))
                pool.tensor_tensor(zx[:, :, :], zx[:, :, :], sh_x.to_broadcast([P, 2, D]), ALU.add).then_inc(s_z, 1)
                pool.tensor_tensor(zc[:, :, :], zc[:, :, :], sh_c.to_broadcast([P, 2, C]), ALU.add).then_inc(s_z, 1)

            def norm_x2(p):
                g = p.group(2)
                if g is None:
                    return
                par = p.par()
                n2 = rows[:, par, :, D:2 * D]
                pool.wait_ge(s_newton, NEWT * (p.g + 3))
                pool.tensor_tensor(n2, rows[:, par, :, 0:D], rstd[:, 4:6].unsqueeze(2).to_broadcast([P, 2, D]),
                                   ALU.mult).then_inc(s_n2m, 1)
                pool.wait_ge(s_n2m, p.g - 1)
                pool.tensor_tensor(n2, n2, shift[:, 4:6].unsqueeze(2).to_broadcast([P, 2, D]),
                                   ALU.add).then_inc(s_n2, 1)

            def split_in(p):
                g = p.group(-2)
                if g is None:
                    return
                par = p.par()
                pool.wait_ge(s_xf, 2 * (p.g + 3))
                if not (p.fixed and p.g < 0):
                    pool.wait_ge(s_job, 12 * (p.g + 1))
                pool.tensor_tensor(XT_h[:, par, :], xf[:, :], zero1[:, :].to_broadcast([P, GT]), ALU.add).then_inc(s_hi, 1)
                pool.tensor_tensor(CT_h[:, par, :], cf[:, :], zero1[0:C, :].to_broadcast([C, GT]), ALU.add).then_inc(s_hi, 1)
                pool.wait_ge(s_hi, 2 * (p.g + 3))
                pool.tensor_tensor(XT_l[:, par, :], xf[:, :], XT_h[:, par, :], ALU.subtract).then_inc(s_lo, 1)
                pool.tensor_tensor(CT_l[:, par, :], cf[:, :], CT_h[:, par, :], ALU.subtract).then_inc(s_lo, 1)

            def send(p):
                g = p.group(3)
                if g is None:
                    return
                par = p.par(3)
                pool.wait_ge(s_route, 6 * (p.g - 2))
                if not (p.fixed and p.g < 4):
                    pool.wait_ge(s_tok, p.g - 3)
                pool.tensor_tensor(rows[:, par, :, ROW - 1].bitcast(I32), token[:, :],
                                   zero1[:, :].bitcast(I32).to_broadcast([P, 2]), ALU.add).then_inc(s_id, 1)
                pool.wait_ge(s_place, 3 * (p.g - 2))
                pool.wait_ge(s_id, p.g - 2)
                pool.tensor_tensor(token[:, :], token[:, :], token_step[:, :], ALU.add).then_inc(s_tok, 1)
                for t in range(2):
                    pool.indirect_dma_start(rows_dram, bass.IndirectOffsetOnAxis(place_i[:, par, t:t + 1], 0),
                                            rows[:, par, t, :], None).then_inc(s_scat[par], 16)

            def step(p):
                if p.odd:
                    split_in(p)
                    send(p)
                else:
                    norm_in(p)
                    norm_x2(p)

            for g in (-2, -1):
                q = Plan(-1, 2 * (g + 2))
                norm_in(q)
                split_in(q)
            run(pool, step)

            def send_out(t, i, trips):
                pool.wait_ge(f_out, t + 1)
                pool.sem_inc(f_send, 1)
                pool.indirect_dma_start(out_rows, bass.IndirectOffsetOnAxis(tile_token[:, i:i + 1], 0),
                                        tile_out[i], None, bounds_check=TOK - 1, oob_is_err=False).then_inc(f_scat[i], 16)

            with pool.Fori(0, TILES // RING) as v:
                for i in range(RING):
                    send_out(v * RING + i, i, v)
            for i in range(RING):
                pool.wait_ge(f_scat[i], 16 * (TILES // RING))

        @block.scalar
        def _(act):
            small = ((gx_col[:, :], g_x.rearrange("(p a) -> p a", a=1)), (bx_col[:, :], b_x.rearrange("(p a) -> p a", a=1)),
                     (gc_col[:, :], g_c.rearrange("(p a) -> p a", a=1)), (bc_col[:, :], b_c.rearrange("(p a) -> p a", a=1)),
                     (gates[:, 0:1], g_xattn.rearrange("(p a) -> p a", a=1).to_broadcast([P, 1])),
                     (gates[:, 1:2], g_ffn.rearrange("(p a) -> p a", a=1).to_broadcast([P, 1])),
                     (rw_sb[:, :], router_w))
            for dst, src in small:
                act.dma_start(dst, src).then_inc(s_small, 16)
            act.wait_ge(s_small, 16 * len(small))
            act.activation(tanhs[:, :], gates[:, :], ACT.Tanh).then_inc(s_tanh, 1)

            def weight_high(i, dst, raw):
                act.activation(dst, raw, ACT.Copy).then_inc(s_wh, 1)

            def prep(p):
                if p.group(-2) is None:
                    return
                act.wait_ge(s_prep, p.g + 3)
                if not (p.fixed and p.g < -1):
                    act.wait_ge(s_lo, 2 * (p.g + 2))
                act.activation(xf[:, :], psM[:, 0:GT], ACT.Identity, bias=bx_col[:, :], scale=gx_col[:, :]).then_inc(s_xf, 1)
                act.activation(cf[:, :], psM[0:C, GT:2 * GT], ACT.Identity, bias=bc_col[:, :], scale=gc_col[:, :]).then_inc(s_xf, 1)

            def job(p, n):
                if p.group(-1) is None:
                    return
                par = p.par(-1)
                act.wait_ge(s_job, 12 * (p.g + 1) + n + 1)
                if n < 4:
                    dst = QT[:, par, 2 * n:2 * n + 2, :].rearrange("p m t -> p (m t)")
                elif n == 4 or 7 <= n <= 9:
                    m = 0 if n == 4 else n - 6
                    dst = KT[:, par, 2 * m:2 * m + 2, :].rearrange("p m t -> p (m t)")
                else:
                    pr, half = (0, n - 5) if n < 7 else (1, n - 10)
                    dst = V[:, par, pr, 512 * half:512 * half + 512]
                act.activation(dst, psJ[n % 2][:, :], ACT.Copy).then_inc(s_jobev, 1)

            def values_high(p):
                s = p.pair(2)
                if s is None:
                    return
                act.wait_ge(s_pv, p.s - 1)
                dst = OT_h[:, :, (p.k % 2) * P:(p.k % 2 + 1) * P].rearrange("p m (b q) -> p b m q", b=2)
                act.activation(dst, psO[:, :].rearrange("p (b m q) -> p b m q", b=2, m=M8), ACT.Copy).then_inc(s_oh, 1)

            def probs_out(p, half):
                if p.pair(1) is None:
                    return
                act.wait_ge(s_pt, 2 * (p.s - 1) + half + 1)
                act.activation(PTs[:, half, :], psT[:, :], ACT.Copy).then_inc(s_ptev, 1)

            def expo(p):
                if p.pair(0) is None:
                    return
                act.wait_ge(s_sub, p.s + 1)
                act.activation(probs[:, p.k % 2, :, :], probs[:, p.k % 2, :, :], ACT.Exp, scale=SCALE).then_inc(s_exp, 1)

            def attn_out(p):
                if p.group(1) is None:
                    return
                act.wait_ge(s_oproj, p.g)
                act.activation(aT[:, :], psM[:, 0:GT], ACT.Copy, scale=tanhs[:, 0:1]).then_inc(s_aT, 1)

            def norm_T(p):
                if p.group(2) is None:
                    return
                act.wait_ge(s_postb, p.g - 1)
                act.activation(n2T[:, :], psM[:, 0:GT], ACT.Copy).then_inc(s_n2T, 1)

            def route_exp(p):
                if p.group(3) is None:
                    return
                act.wait_ge(s_dl, p.g - 2)
                act.activation(el[:, :, :], dl[:, :, :], ACT.Exp).then_inc(s_el, 1)

            def step(p):
                if p.odd:
                    job(p, 7)
                    job(p, 8)
                    job(p, 9)
                    expo(p)
                    norm_T(p)
                    values_high(p)
                    job(p, 10)
                    probs_out(p, 0)
                    prep(p)
                    job(p, 11)
                    probs_out(p, 1)
                    attn_out(p)
                else:
                    job(p, 0)
                    job(p, 1)
                    route_exp(p)
                    job(p, 2)
                    expo(p)
                    values_high(p)
                    job(p, 3)
                    probs_out(p, 0)
                    job(p, 4)
                    job(p, 5)
                    probs_out(p, 1)
                    job(p, 6)

            for i, (dst, raw) in enumerate(((Wq_h[:, :], raw_q), (Wk_h[:, :], raw_k), (Wv_h[:, :], raw_v),
                                            (Wo_h[:, :, :].rearrange("p m d -> p (m d)"), raw_o))):
                if i == 0:
                    act.wait_ge(s_raw, 64)
                weight_high(i, dst, raw)
            for g in (-2, -1):
                prep(Plan(-1, 2 * (g + 2)))
            for n in range(12):
                job(Plan(-1, 2), n)
            run(act, step)

            def ffn(t, v, i, on, entry):
                if on[0]:
                    act.wait_ge(f_t1, t + 1)
                    act.activation(n2_T[i % 2], psJ[i % 2][:, 0:P], ACT.Copy).then_inc(f_t1ev, 1)
                if on[1]:
                    b = (i - 1) % 2
                    at = entry[1]
                    act.wait_ge(f_w1, t)
                    if not (isinstance(t, int) and t < 3):
                        act.wait_ge(f_w2, t - 2)
                    for k in range(FK):
                        act.activation(hid_T[b][:, P * k:P * k + P], (psM, psT)[b][:, P * k:P * k + P], ACT.Gelu,
                                       bias=b1_sb[:, bass.ds(at + k, 1)]).then_inc(f_gelu, 1)

            act.activation(gelu_warm[:, :], zero1[:, :], ACT.Gelu)
            act.wait_ge(s_b1T, 1)
            act.activation(b1_sb[:, :], psT[:, 0:E * FK], ACT.Copy).then_inc(s_b1, 1)
            act.wait_ge(s_b1, 1)
            act.wait_ge(s_tab, 1)
            ffn_run(act, mybir.EngineType.Activation, k_tab, (E - 1) * FK, ffn)

        @block.tensor
        def _(pe):
            misc = [None]

            def misc_free():
                if misc[0] is not None:
                    pe.wait_ge(*misc[0])

            def split3(outs, w_h, w_l, r_h, r_l):
                return [lambda: pe.matmul(outs, w_h, r_h, start=True, stop=False),
                        lambda: pe.matmul(outs, w_h, r_l, start=False, stop=False),
                        lambda: pe.matmul(outs, w_l, r_h, start=False, stop=True)]

            def prep(p):
                if p.group(-2) is None:
                    return
                misc_free()
                pe.wait_ge(s_z, 2 * (p.g + 3))
                for t in range(2):
                    pe.transpose(psM[:, P * t:P * t + P], zx[:, t, :], ident[:, :])
                for t in range(2):
                    last = pe.transpose(psM[0:C, GT + P * t:GT + P * t + P], zc[:, t, :], ident[:, :])
                last.then_inc(s_prep, 1)
                misc[0] = (s_xf, 2 * (p.g + 3))

            def job(p, n, half=None, ahead=None):
                if p.group(-1) is None:
                    if ahead:
                        ahead()
                    return
                par = p.par(-1)
                bank = psJ[n % 2]
                if half != 1:
                    if n == 0:
                        pe.wait_ge(s_lo, 2 * (p.g + 2))
                    if not (p.fixed and 12 * (p.g + 1) + n < 2):
                        pe.wait_ge(s_jobev, 12 * (p.g + 1) + n - 1)
                if n < 5 or 7 <= n <= 9:
                    w_h, w_l, r_h, r_l = (Wq_h, Wq_l, XT_h, XT_l) if n < 4 else (Wk_h, Wk_l, CT_h, CT_l)
                    m0 = 2 * n if n < 4 else 0 if n == 4 else 2 * (n - 6)
                    products = []
                    for i in range(2):
                        cols = slice((m0 + i) * P, (m0 + i + 1) * P)
                        products += split3(bank[:, GT * i:GT * i + GT], w_h[:, cols], w_l[:, cols], r_h[:, par, :], r_l[:, par, :])
                    middle = 3
                else:
                    pr, h = (0, n - 5) if n < 7 else (1, n - 10)
                    tok, cols = slice(pr * P, pr * P + P), slice(512 * h, 512 * h + 512)
                    products = split3(bank[:, :], CT_h[:, par, tok], CT_l[:, par, tok], Wv_h[:, cols], Wv_l[:, cols])
                    middle = 2
                products = {None: products, 0: products[:middle], 1: products[middle:]}[half]
                for product in products[:-1]:
                    product()
                if ahead:
                    ahead()
                last = products[-1]()
                if half != 0:
                    last.then_inc(s_job, 1)

            def scores(p, part_of_4):
                if p.pair(0) is None:
                    return
                tok = (p.k % 2) * P
                for g in range(HG // 4 * part_of_4, HG // 4 * (part_of_4 + 1)):
                    for b in range(2):
                        for c in range(2):
                            for r in range(2):
                                part = slice(64 * r, 64 * r + 64)
                                m = 2 * g + c
                                col = 512 * r + (2 * g + b) * SEQ
                                cols = slice(tok + SEQ * b, tok + SEQ * b + SEQ)
                                last = pe.matmul(psS[64 * c:64 * c + 64, col:col + SEQ],
                                                 QT[part, p.par(), m, cols], KT[part, p.par(), m, cols],
                                                 start=True, stop=True)
                if part_of_4 == 3:
                    last.then_inc(s_qk, 1)

            def value_sums(p, part_of_4):
                if p.pair(2) is None:
                    return
                for m in range(M8 // 4 * part_of_4, M8 // 4 * (part_of_4 + 1)):
                    for h in range(2):
                        for b in range(2):
                            part = slice(64 * b, 64 * b + 64)
                            head = 2 * m + h
                            col = 512 * b + m * SEQ
                            last = pe.matmul(psO[64 * h:64 * h + 64, col:col + SEQ],
                                             V[part, p.par(1), p.k % 2, head * DH:head * DH + DH],
                                             PTs[part, h, m * SEQ:(m + 1) * SEQ],
                                             start=True, stop=True)
                if part_of_4 == 3:
                    last.then_inc(s_pv, 1)

            def scores_ready(p):
                s = p.s + 1
                if p.fixed and s >= PAIRS:
                    return
                if not (p.fixed and s < 1):
                    pe.wait_ge(s_sub, s)
                if p.odd:
                    pe.wait_ge(s_jobev, 12 * (p.g + 1) + 10)

            def sums_ready(p):
                if p.pair(2) is None:
                    return
                pe.wait_ge(s_ptev, 2 * (p.s - 1))
                if not (p.fixed and p.s < 3):
                    pe.wait_ge(s_ol, p.s - 2)

            def probs_T(p, half):
                if p.pair(1) is None:
                    return
                if half == 0:
                    pe.wait_ge(s_norm, p.s)
                if not (p.fixed and 2 * (p.s - 1) + half < 1):
                    pe.wait_ge(s_ptev, 2 * (p.s - 1) + half)
                for g in range(HG):
                    src = probs[:, (p.k - 1) % 2, 8 * half + 2 * g:8 * half + 2 * g + 2, :].rearrange("p b k -> p (b k)")
                    last = pe.transpose(psT[:, P * g:P * g + P], src, ident[:, :])
                last.then_inc(s_pt, 1)

            def out_proj(p, ahead):
                if p.group(1) is None:
                    ahead()
                    return
                misc_free()
                pe.wait_ge(s_oh, 2 * p.g)
                for m in range(M8):
                    pe.matmul(psM[:, 0:GT], Wo_h[:, m, :], OT_h[:, m, :], start=(m == 0), stop=False)
                    pe.matmul(psM[:, 0:GT], Wo_l[:, m, :], OT_h[:, m, :], start=False, stop=False)
                pe.wait_ge(s_ol, 2 * p.g)
                for m in range(M8):
                    if m == M8 - 1:
                        ahead()
                    last = pe.matmul(psM[:, 0:GT], Wo_h[:, m, :], OT_l[:, m, :], start=False, stop=(m == M8 - 1))
                last.then_inc(s_oproj, 1)
                misc[0] = (s_aT, p.g)

            def post_a(p):
                if p.group(2) is None:
                    return
                misc_free()
                pe.wait_ge(s_aT, p.g - 1)
                for t in range(2):
                    last = pe.transpose(psM[:, P * t:P * t + P], aT[:, P * t:P * t + P], ident[:, :])
                last.then_inc(s_posta, 1)
                misc[0] = (s_x2, p.g - 1)

            def post_b(p):
                if p.group(2) is None:
                    return
                misc_free()
                pe.wait_ge(s_n2, p.g - 1)
                for t in range(2):
                    last = pe.transpose(psM[:, P * t:P * t + P], rows[:, p.par(), t, D:2 * D], ident[:, :])
                last.then_inc(s_postb, 1)
                misc[0] = (s_n2T, p.g - 1)

            def router(p):
                if p.group(3) is None:
                    return
                misc_free()
                pe.wait_ge(s_n2T, p.g - 2)
                for t in range(2):
                    last = pe.matmul(psM[:, E * t:E * t + E], n2T[:, P * t:P * t + P], rw_sb[:, :], start=True, stop=True)
                last.then_inc(s_logit, 1)
                misc[0] = (s_dl, p.g - 2)

            def rank(p):
                if p.group(3) is None:
                    return
                misc_free()
                pe.wait_ge(s_hot, p.g - 2)
                pe.matmul(psM[:, 0:E], before[:, :], onehot[:, 0, :], start=True, stop=True)
                pe.matmul(psM[:, E:2 * E], ones_b[:, :], onehot[:, 0, :], start=True, stop=False)
                pe.matmul(psM[:, E:2 * E], before[:, :], onehot[:, 1, :], start=False, stop=True)
                pe.matmul(psM[:, 2 * E:3 * E], ones_b[:, :], onehot[:, 0, :], start=True, stop=False)
                pe.matmul(psM[:, 2 * E:3 * E], ones_b[:, :], onehot[:, 1, :], start=False, stop=True).then_inc(s_rank, 1)
                misc[0] = (s_ranked, p.g - 2)

            def step(p):
                if p.k == 0:
                    misc[0] = (s_aT, p.g - 1) if p.group(2) is not None else misc[0]
                if p.odd:
                    scores(p, 0)
                    job(p, 7, 0)
                    scores(p, 1)
                    job(p, 7, 1)
                    scores(p, 2)
                    job(p, 8, 0)
                    scores(p, 3)
                    job(p, 8, 1, lambda: sums_ready(p))
                    value_sums(p, 0)
                    job(p, 9, 0)
                    value_sums(p, 1)
                    job(p, 9, 1)
                    value_sums(p, 2)
                    job(p, 10, 0)
                    post_b(p)
                    value_sums(p, 3)
                    job(p, 10, 1)
                    probs_T(p, 0)
                    job(p, 11, 0)
                    prep(p)
                    job(p, 11, 1)
                    probs_T(p, 1)
                    out_proj(p, lambda: scores_ready(p))
                else:
                    scores(p, 0)
                    job(p, 0, 0)
                    scores(p, 1)
                    job(p, 0, 1)
                    router(p)
                    scores(p, 2)
                    job(p, 1, 0)
                    scores(p, 3)
                    job(p, 1, 1, lambda: sums_ready(p))
                    value_sums(p, 0)
                    job(p, 2, 0)
                    post_a(p)
                    value_sums(p, 1)
                    job(p, 2, 1)
                    value_sums(p, 2)
                    job(p, 3, 0)
                    value_sums(p, 3)
                    job(p, 3, 1)
                    probs_T(p, 0)
                    job(p, 4)
                    job(p, 5, 0)
                    rank(p)
                    job(p, 5, 1)
                    probs_T(p, 1)
                    job(p, 6, ahead=lambda: scores_ready(p))

            pe.wait_ge(s_cc, 2)
            prep(Plan(-1, 0))
            prep(Plan(-1, 2))
            pe.wait_ge(s_wl, 4)
            for n in range(12):
                job(Plan(-1, 2), n)
            pe.wait_ge(s_jobev, 10)
            run(pe, step)

            def ffn(t, v, i, on, entry):
                if on[0]:
                    if not (isinstance(t, int) and t < 2):
                        pe.wait_ge(f_t1ev, t - 1)
                    pe.wait_ge(f_load[i], 16 * (v + 1))
                    pe.transpose(psJ[i % 2][:, 0:P], tile_rows[i][:, D:2 * D], ident[:, :]).then_inc(f_t1, 1)
                if on[1]:
                    b = (i - 1) % 2
                    pe.wait_ge(f_t1ev, t)
                    pe.wait_ge(f_pick, t)
                    if not (isinstance(t, int) and t < 3):
                        pe.wait_ge(f_gelu, FK * (t - 2))
                    for k in range(FK):
                        last = pe.matmul((psM, psT)[b][:, P * k:P * k + P], w1_tile[b][:, P * k:P * k + P],
                                         n2_T[b], start=True, stop=True)
                    last.then_inc(f_w1, 1)
                if on[2]:
                    at = entry[2]
                    o = 512 * (i % 2)
                    pe.wait_ge(f_gelu, FK * (t - 1))
                    if not (isinstance(t, int) and t < 4):
                        pe.wait_ge(f_sum, t - 3)
                    for k in range(FK):
                        last = pe.matmul(psO[:, o:o + D], hid_T[i % 2][:, P * k:P * k + P],
                                         w2_sb[:, bass.ds(at + k * D, D)], start=(k == 0), stop=(k == FK - 1))
                    last.then_inc(f_w2, 1)

            pe.wait_ge(s_bias, 32)
            pe.wait_ge(s_ptev, 2 * PAIRS)
            pe.transpose(psT[:, 0:E * FK], b1_rows[:, :], ident[0:E * FK, 0:E * FK]).then_inc(s_b1T, 1)
            pe.wait_ge(s_cols, 6)
            for i in range(4):
                last = pe.transpose(psM[0:1, P * i:P * i + P], t_cols[:, i:i + 1], ident[:, :])
            last.then_inc(s_tabT, 1)
            pe.wait_ge(s_ffn, 32)
            pe.wait_ge(s_b1, 1)
            pe.wait_ge(s_tab, 1)
            ffn_run(pe, mybir.EngineType.PE, f_tab, (E - 1) * F, ffn)

        @block.vector
        def _(dve):
            def stats_in(p):
                if p.group(-2) is None:
                    return
                par = p.par()
                dve.wait_ge(s_in[par], 32 * p.uses(-2))
                if not (p.fixed and p.g < -1):
                    dve.wait_ge(s_agg, 4 * (p.g + 2))
                for t in range(2):
                    dve.bn_stats(bn6[:, t, :], x_in[:, par, t, :]).then_inc(s_stat, 1)
                for t in range(2):
                    dve.bn_stats(bn6[:, 2 + t, :], c_in[:, par, t, :]).then_inc(s_stat, 1)

            def stats_in_done(p):
                if p.group(-2) is not None:
                    dve.wait_ge(s_stat, 4 * (p.g + 3))
                    if not (p.fixed and p.g < -1):
                        dve.wait_ge(s_newton, NEWT * (p.g + 2))

            def means_in(p):
                if p.group(-2) is None:
                    return
                for t in range(4):
                    dve.bn_aggr(mv[:, t, :], bn6[:, t, :]).then_inc(s_agg, 1)

            def roots(p):
                if p.group(-2) is None and p.group(2) is None:
                    return
                n = NEWT * (p.g + 2)
                if p.group(-2) is not None:
                    dve.wait_ge(s_agg, 4 * (p.g + 3))
                if p.group(2) is not None:
                    dve.wait_ge(s_agg2, 2 * (p.g - 1))
                dve.tensor_tensor(nw[:, :], mv[:, :, 1], var_mul[:, :], ALU.mult).then_inc(s_newton, 1)
                dve.wait_ge(s_newton, n + 1)
                dve.tensor_tensor(nw[:, :], nw[:, :], var_add[:, :], ALU.add).then_inc(s_newton, 1)
                dve.wait_ge(s_newton, n + 2)
                if not (p.fixed and p.g < -1):
                    if not (p.fixed and p.g + 1 >= GROUPS):
                        dve.wait_ge(s_z, 2 * (p.g + 2))
                if not (p.fixed and not 0 <= p.g - 3 < GROUPS):
                    dve.wait_ge(s_n2, p.g - 2)
                dve.tensor_scalar(rstd[:, :].bitcast(I32), nw[:, :].bitcast(I32), -0.5, RSQRT_SEED,
                                  ALU.mult, ALU.add).then_inc(s_newton, 1)
                n += 3
                for _ in range(NEWTON):
                    dve.wait_ge(s_newton, n)
                    dve.tensor_tensor(nq[:, :], rstd[:, :], rstd[:, :], ALU.mult).then_inc(s_newton, 1)
                    dve.wait_ge(s_newton, n + 1)
                    dve.scalar_tensor_tensor(nq[:, :], nq[:, :], -0.5, nw[:, :], ALU.mult, ALU.mult).then_inc(s_newton, 1)
                    dve.wait_ge(s_newton, n + 2)
                    dve.scalar_tensor_tensor(rstd[:, :], nq[:, :], 1.5, rstd[:, :], ALU.add, ALU.mult).then_inc(s_newton, 1)
                    n += 3
                dve.wait_ge(s_newton, n)
                dve.scalar_tensor_tensor(shift[:, :], mv[:, :, 0], -1.0, rstd[:, :], ALU.mult, ALU.mult).then_inc(s_newton, 1)

            def scores_max(p):
                if p.pair(0) is None:
                    return
                dve.wait_ge(s_qk, p.s + 1)
                dve.tensor_reduce(row_max[:, :], psS[:, :].rearrange("p (n k) -> p n k", k=SEQ), AX.X,
                                  ALU.max).then_inc(s_max, 1)

            def scores_sub(p):
                if p.pair(0) is None:
                    return
                dve.wait_ge(s_max, p.s + 1)
                dve.tensor_tensor(probs[:, p.k % 2, :, :], psS[:, :].rearrange("p (n k) -> p n k", k=SEQ),
                                  row_max[:, :].unsqueeze(2).to_broadcast([P, 16, SEQ]), ALU.subtract).then_inc(s_sub, 1)

            def sums(p):
                if p.pair(0) is None:
                    return
                pr = probs[:, p.k % 2, :, :]
                dve.wait_ge(s_exp, p.s + 1)
                dve.tensor_reduce(row_sum[:, :], pr, AX.X, ALU.add).then_inc(s_sum, 1)
                dve.wait_ge(s_sum, p.s + 1)
                dve.reciprocal(row_inv[:, :], row_sum[:, :]).then_inc(s_inv, 1)

            def normalise(p):
                if p.pair(0) is None:
                    return
                pr = probs[:, p.k % 2, :, :]
                dve.wait_ge(s_inv, p.s + 1)
                dve.tensor_tensor(pr, pr, row_inv[:, :].unsqueeze(2).to_broadcast([P, 16, SEQ]), ALU.mult).then_inc(s_norm, 1)

            def values_low(p):
                if p.pair(2) is None:
                    return
                cols = slice((p.k % 2) * P, (p.k % 2 + 1) * P)
                hi = OT_h[:, :, cols].rearrange("p m (b q) -> p b m q", b=2)
                lo = OT_l[:, :, cols].rearrange("p m (b q) -> p b m q", b=2)
                dve.wait_ge(s_oh, p.s - 1)
                dve.tensor_tensor(lo, psO[:, :].rearrange("p (b m q) -> p b m q", b=2, m=M8), hi,
                                  ALU.subtract).then_inc(s_ol, 1)

            def residual(p):
                if p.group(2) is None:
                    return
                par = p.par()
                dve.wait_ge(s_res[par], 16 * p.uses(2))
                if not (p.fixed and p.g < 4):
                    dve.wait_ge(s_scat[par], 32 * p.uses(4))
                    dve.wait_ge(s_agg2, 2 * (p.g - 2))
                dve.wait_ge(s_posta, p.g - 1)
                dve.tensor_tensor(rows[:, par, :, 0:D], psM[:, 0:GT].rearrange("p (t d) -> p t d", t=2),
                                  x_res[:, par, :, :], ALU.add).then_inc(s_x2, 1)
                dve.wait_ge(s_x2, p.g - 1)
                for t in range(2):
                    dve.bn_stats(bn6[:, 4 + t, :], rows[:, par, t, 0:D]).then_inc(s_stat2, 1)

            def residual_done(p):
                if p.group(2) is not None:
                    dve.wait_ge(s_stat2, 2 * (p.g - 1))

            def means_x2(p):
                if p.group(2) is None:
                    return
                for t in range(2):
                    dve.bn_aggr(mv[:, 4 + t, :], bn6[:, 4 + t, :]).then_inc(s_agg2, 1)

            def route(p):
                if p.group(3) is None:
                    return
                n, par = 6 * (p.g - 3), p.par(3)
                logits = psM[:, 0:2 * E].rearrange("p (t e) -> p t e", t=2)
                dve.wait_ge(s_logit, p.g - 2)
                dve.tensor_reduce(lmax[:, :], logits, AX.X, ALU.max).then_inc(s_lmax, 1)
                dve.wait_ge(s_lmax, p.g - 2)
                dve.tensor_tensor(dl[:, :, :], logits, lmax[:, :].unsqueeze(2).to_broadcast([P, 2, E]),
                                  ALU.subtract).then_inc(s_dl, 1)
                dve.wait_ge(s_dl, p.g - 2)
                dve.tensor_scalar(cand[:, :, :], dl[:, :, :], 0.0, 2.0 * E, ALU.is_lt, ALU.mult).then_inc(s_route, 1)
                dve.wait_ge(s_route, n + 1)
                dve.tensor_tensor(cand[:, :, :], cand[:, :, :], e_iota[:, :, :], ALU.add).then_inc(s_route, 1)
                dve.wait_ge(s_route, n + 2)
                dve.tensor_reduce(first[:, :], cand[:, :, :], AX.X, ALU.min).then_inc(s_route, 1)
                dve.wait_ge(s_route, n + 3)
                dve.tensor_tensor(onehot[:, :, :], e_iota[:, :, :], first[:, :].unsqueeze(2).to_broadcast([P, 2, E]),
                                  ALU.is_equal).then_inc(s_hot, 1)

            def weight(p):
                if p.group(3) is None:
                    return
                n, par = 6 * (p.g - 3), p.par(3)
                dve.wait_ge(s_el, p.g - 2)
                dve.tensor_reduce(den[:, :], el[:, :, :], AX.X, ALU.add).then_inc(s_route, 1)
                dve.wait_ge(s_route, n + 4)
                dve.reciprocal(inv[:, :], den[:, :]).then_inc(s_route, 1)
                dve.wait_ge(s_route, n + 5)
                dve.tensor_scalar(rows[:, par, :, 2 * D], inv[:, :], tanhs[:, 1:2], None, ALU.mult).then_inc(s_route, 1)

            def places(p):
                if p.group(3) is None:
                    return
                n, par = 3 * (p.g - 3), p.par(3)
                dve.wait_ge(s_rank, p.g - 2)
                if not (p.fixed and p.g < 4):
                    dve.wait_ge(s_ranked, p.g - 3)
                dve.tensor_tensor(place[:, :, :], psM[:, 0:2 * E].rearrange("p (t e) -> p t e", t=2),
                                  next_row[:, :].unsqueeze(1).to_broadcast([P, 2, E]), ALU.add).then_inc(s_place, 1)
                dve.wait_ge(s_place, n + 1)
                dve.tensor_tensor(next_row[:, :], next_row[:, :], psM[:, 2 * E:3 * E], ALU.add).then_inc(s_ranked, 1)
                dve.tensor_tensor(place[:, :, :], place[:, :, :], onehot[:, :, :], ALU.mult).then_inc(s_place, 1)
                dve.wait_ge(s_place, n + 2)
                with nc.allow_low_precision(reason="whole numbers below 2**24"):
                    dve.tensor_reduce(place_i[:, par, :], place[:, :, :], AX.X, ALU.add).then_inc(s_place, 1)

            def step(p):
                if p.odd:
                    scores_max(p)
                    scores_sub(p)
                    sums(p)
                    values_low(p)
                    normalise(p)
                else:
                    stats_in(p)
                    route(p)
                    scores_max(p)
                    stats_in_done(p)
                    scores_sub(p)
                    means_in(p)
                    residual(p)
                    residual_done(p)
                    sums(p)
                    means_x2(p)
                    values_low(p)
                    normalise(p)
                    places(p)
                    weight(p)
                    roots(p)

            dve.wait_ge(s_const, 17)
            dve.tensor_copy(e_iota[:, :, :], e_int[:, :, :])
            dve.tensor_copy(next_row[:, :], r_int[:, :])
            dve.tensor_copy(t_f[:, :], t_int[:, :]).then_inc(s_link, 1)
            for g in (-2, -1):
                q = Plan(-1, 2 * (g + 2))
                stats_in(q)
                stats_in_done(q)
                means_in(q)
                roots(q)
                if g == -2:
                    for i, (lo, hi, raw) in enumerate(((Wq_l[:, :], Wq_h[:, :], raw_q), (Wk_l[:, :], Wk_h[:, :], raw_k),
                                                       (Wv_l[:, :], Wv_h[:, :], raw_v),
                                                       (Wo_l[:, :, :].rearrange("p m d -> p (m d)"),
                                                        Wo_h[:, :, :].rearrange("p m d -> p (m d)"), raw_o))):
                        dve.wait_ge(s_wh, i + 1)
                        dve.tensor_tensor(lo, raw, hi, ALU.subtract).then_inc(s_wl, 1)
            dve.wait_ge(s_tanh, 1)
            dve.wait_ge(s_link, 1)
            run(dve, step)

            def link(ins, n):
                ins.then_inc(s_link, 1)
                dve.wait_ge(s_link, n)

            dve.wait_ge(s_ranked, GROUPS)
            link(dve.tensor_tensor(n_tiles[:, :], next_row[:, :], r_int[:, :], ALU.subtract), 2)
            link(dve.tensor_scalar(ends_i[:, :], n_tiles[:, :], float(P - 1), None, ALU.add), 3)
            link(dve.tensor_scalar(ends_i[:, :], ends_i[:, :], 7, None, ALU.logical_shift_right), 4)
            link(dve.tensor_copy(n_tiles[:, :], ends_i[:, :]), 5)
            dve.tensor_tensor_scan(cum[:, :], one14[:, :], n_tiles[:, :], 0.0, ALU.mult, ALU.add).then_inc(s_link, 1)
            dve.tensor_tensor(move[:, 0:E - 1], next_row[:, 1:E], next_row[:, 0:E - 1], ALU.subtract).then_inc(s_link, 1)
            link(dve.tensor_tensor(t_base[:, :], t_f[:, 1:2], next_row[:, 0:1], ALU.add), 8)
            dve.scalar_tensor_tensor(move[:, :], n_tiles[:, :], float(P), move[:, :], ALU.mult, ALU.add).then_inc(s_link, 1)
            link(dve.tensor_scalar(past[:, :], cum[:, :], t_f[:, 0:1], None, ALU.is_le), 10)
            dve.tensor_reduce(t_expert[:, :], past[:, :], AX.X, ALU.add).then_inc(s_link, 1)
            link(dve.tensor_tensor(past_move[:, :], past[:, :], move[:, :], ALU.mult), 12)
            link(dve.tensor_reduce(t_row[:, :], past_move[:, :], AX.X, ALU.add), 13)
            for i, size in ((1, F), (2, D), (3, FK)):
                dve.tensor_scalar(t_cols[:, i:i + 1], t_expert[:, :], float(E - 1), float(size), ALU.min,
                                  ALU.mult).then_inc(s_cols, 1)
            dve.tensor_tensor(t_row[:, :], t_row[:, :], t_base[:, :], ALU.add).then_inc(s_cols, 1)
            dve.wait_ge(s_cols, 4)
            dve.tensor_scalar(t_cols[:, 0:1], t_row[:, :], float(E * REGION), None, ALU.min).then_inc(s_cols, 2)
            dve.wait_ge(s_tabT, 1)
            dve.tensor_copy(table[:, :, :].rearrange("a c t -> a (c t)"), psM[0:1, :]).then_inc(s_tab, 1)

            def ffn(t, v, i, on, entry):
                if on[0]:
                    at = entry[0] * FK
                    if not (isinstance(t, int) and t < 2):
                        dve.wait_ge(f_w1, t - 1)
                    dve.tensor_copy(w1_tile[i % 2], w1_sb[:, bass.ds(at, F)]).then_inc(f_pick, 1)
                if on[2]:
                    r = (i - 2) % RING
                    o = 512 * (i % 2)
                    at = entry[2]
                    if not (isinstance(t, int) and t < 3):
                        dve.wait_ge(f_out, t - 2)
                    dve.wait_ge(f_w2, t - 1)
                    dve.tensor_tensor(ysum[:, :], psO[:, o:o + D], b2_sb[:, bass.ds(at, D)], ALU.add).then_inc(f_sum, 1)
                    if not (isinstance(t, int) and t - 2 < RING):
                        dve.wait_ge(f_scat[r], 16 * (v + (i - 2) // RING))
                    dve.tensor_copy(tile_token[:, r:r + 1], tile_rows[r][:, ROW - 1:ROW].bitcast(I32))
                    dve.wait_ge(f_sum, t - 1)
                    dve.scalar_tensor_tensor(tile_out[r], ysum[:, :], tile_rows[r][:, 2 * D:2 * D + 1],
                                             tile_rows[r][:, 0:D], ALU.mult, ALU.add).then_inc(f_out, 1)

            dve.wait_ge(s_ffn, 32)
            dve.wait_ge(s_bias, 32)
            dve.wait_ge(s_tab, 1)
            ffn_run(dve, mybir.EngineType.DVE, d_tab, (E - 1) * D, ffn)


_INS = ['x', 'ctx_768', 'g_xattn', 'g_ffn', 'L0_xattn_g_x', 'L0_xattn_b_x', 'L0_xattn_g_c', 'L0_xattn_b_c',
        'L0_xattn_Wq', 'L0_xattn_Wk', 'L0_xattn_Wv', 'L0_xattn_Wo', 'L0_ffn_router_w', 'L0_ffn_w1', 'L0_ffn_b1',
        'L0_ffn_w2', 'L0_ffn_b2']


def kernel(**inputs):
    import numpy as _np
    import concourse.bacc as _bacc
    from concourse import mybir as _mybir
    from concourse.bass_utils import run_bass_kernel_spmd as _run

    nc = _bacc.Bacc("TRN2", target_bir_lowering=False, num_devices=1)
    arrays, args = {}, []
    for name in _INS:
        a = _np.ascontiguousarray(inputs[name])
        arrays[f"in_{name}_dram"] = a
        args.append(nc.dram_tensor(f"in_{name}_dram", a.shape, _mybir.dt.from_np(a.dtype), kind="ExternalInput").ap())
    shape = tuple(inputs['x'].shape)
    args.append(nc.dram_tensor("out_dram", shape, _mybir.dt.from_np(_np.dtype('float32')), kind="ExternalOutput").ap())
    gated_block_kernel(nc, *args)
    r = _run(nc, [arrays], core_ids=[0])
    return r.results[0]["out_dram"]
```

```python
from contextlib import ExitStack

import concourse.bass as bass
from concourse import mybir

F32 = mybir.dt.float32
F32R = mybir.dt.float32r
BF16 = mybir.dt.bfloat16
I32 = mybir.dt.int32
ALU = mybir.AluOpType
ACT = mybir.ActivationFunctionType
AX = mybir.AxisListType

P = 128
SEQ = 64
DH = 64
EPS = 1e-5
SCALE = float(DH) ** -0.5
RSQRT_SEED = float(0x5F3759DF)
NEWTON = 3
LOOP_FROM, LOOP_TO = 2, 14
RING = 16
SLOTS = 16
PACK = 4


def gated_block_kernel(nc, x, ctx768, g_xattn, g_ffn, g_x, b_x, g_c, b_c, Wq, Wk, Wv, Wo,
                       router_w, w1, b1, w2, b2, out):
    B, N, D = x.shape
    C = ctx768.shape[2]
    INNER = Wq.shape[1]
    H = INNER // DH
    M8 = INNER // P
    HG = H // 4
    E, _, F = w1.shape
    FK = F // P
    TOK = B * N
    GT = 2 * P
    GROUPS = TOK // GT
    PAIRS = TOK // P
    REGION = P + TOK
    ROW = D + D + 2
    TILES = -(-(TOK // P + E - 1) // RING) * RING
    assert E <= SLOTS and RING % PACK == 0
    assert N == SEQ and D == P and GROUPS == 2 * (LOOP_TO + 2)

    rows_dram = nc.dram_tensor("rows_by_expert", [E * REGION + P, ROW], F32, kind="Internal").ap()

    x_t = x.rearrange("b n d -> (b n) d").rearrange("(g j p) d -> g p j d", j=2, p=P)
    c_t = ctx768.rearrange("b n d -> (b n) d").rearrange("(g j p) d -> g p j d", j=2, p=P)
    out_rows = out.rearrange("b n d -> (b n) d")

    with ExitStack() as stack:
        def sb(name, shape, dt=F32):
            return stack.enter_context(nc.sbuf_tensor(name, shape, dt))

        def psum(name, shape):
            return stack.enter_context(nc.psum_tensor(name, shape, F32))

        def sem(name):
            return stack.enter_context(nc.semaphore(name))

        Wq_h, Wq_l = sb("Wq_h", [P, INNER], F32R), sb("Wq_l", [P, INNER], F32R)
        Wk_h, Wk_l = sb("Wk_h", [C, INNER], F32R), sb("Wk_l", [C, INNER], F32R)
        Wv_h, Wv_l = sb("Wv_h", [C, INNER], F32R), sb("Wv_l", [C, INNER], F32R)
        Wo_h, Wo_l = sb("Wo_h", [P, M8, D], F32R), sb("Wo_l", [P, M8, D], F32R)
        w1_sb = sb("w1_sb", [P, SLOTS * F])
        w2_sb = sb("w2_sb", [P, SLOTS * F])
        rw_sb = sb("rw_sb", [P, E])
        gx_col, bx_col = sb("gx_col", [P, 1]), sb("bx_col", [P, 1])
        gc_col, bc_col = sb("gc_col", [C, 1]), sb("bc_col", [C, 1])
        gates = sb("gates", [P, 2])
        tanhs = sb("tanhs", [P, 2])
        ident = sb("ident", [P, P])
        before = sb("before", [P, P], BF16)
        ones_b = sb("ones_b", [P, P], BF16)
        zero1 = sb("zero1", [P, 1])
        var_mul, var_add = sb("var_mul", [P, 6]), sb("var_add", [P, 6])
        e_int, e_iota = sb("e_int", [P, 2, E], I32), sb("e_iota", [P, 2, E])
        r_int = sb("r_int", [P, E], I32)
        token = sb("token", [P, 2], I32)
        token_step = sb("token_step", [P, 2], I32)
        x_in, c_in = sb("x_in", [P, 2, 2, D]), sb("c_in", [P, 2, 2, C])
        x_res = sb("x_res", [P, 2, 2, D])
        zx, zc = sb("zx", [P, 2, D]), sb("zc", [P, 2, C])
        xf, cf = sb("xf", [P, GT]), sb("cf", [C, GT])
        XT_h, XT_l = sb("XT_h", [P, 2, GT], F32R), sb("XT_l", [P, 2, GT], F32R)
        CT_h, CT_l = sb("CT_h", [C, 2, GT], F32R), sb("CT_l", [C, 2, GT], F32R)
        QT = sb("QT", [P, 2, M8, GT])
        KT = sb("KT", [P, 2, M8, GT // SEQ, 2, SEQ])
        V = sb("V", [P, 2, 2, INNER])
        probs = sb("probs", [P, 2, 2 * HG * 2, SEQ])
        row_max, row_sum, row_inv = sb("row_max", [P, 16]), sb("row_sum", [P, 16]), sb("row_inv", [P, 16])
        PTs = sb("PTs", [P, 2, 2, M8, 2, SEQ])
        OT_h, OT_l = sb("OT_h", [P, M8, GT], F32R), sb("OT_l", [P, M8, GT], F32R)
        aT = sb("aT", [P, GT])
        rows = sb("rows", [P, 2, 2, ROW])
        n2T = sb("n2T", [P, GT])
        bn6 = sb("bn6", [P, 6, 6])
        mv = sb("mv", [P, 6, 2])
        nw, nq = sb("nw", [P, 6]), sb("nq", [P, 6])
        rstd, shift = sb("rstd", [P, 6]), sb("shift", [P, 6])
        lmax = sb("lmax", [P, 2])
        dl, el, cand = sb("dl", [P, 2, E]), sb("el", [P, 2, E]), sb("cand", [P, 2, E])
        first, den, inv = sb("first", [P, 2]), sb("den", [P, 2]), sb("inv", [P, 2])
        onehot = sb("onehot", [P, 2, E], BF16)
        place = sb("place", [P, 2, E])
        place_i = sb("place_i", [P, 2, 2], I32)
        next_row = sb("next_row", [P, E])
        pad_row = sb("pad_row", [P, ROW])
        ends_i = sb("ends_i", [P, E], I32)
        n_tiles, cum, one14 = sb("n_tiles", [P, E]), sb("cum", [P, E]), sb("one14", [P, E])
        move = sb("move", [P, E])
        past, past_move = sb("past", [P, E]), sb("past_move", [P, E])
        t_int, t_f = sb("t_int", [P, 2], I32), sb("t_f", [P, 2])
        t_expert, t_row, t_base = sb("t_expert", [P, 1]), sb("t_row", [P, 1]), sb("t_base", [P, 1])
        t_cols = sb("t_cols", [P, 2])
        row_tab = sb("row_tab", [1, P], I32)
        packed = sb("packed", [1, P // PACK])
        expert_tab = sb("expert_tab", [1, P // PACK], I32)
        b1_rows = sb("b1_rows", [E * FK, P])
        b1_sb = sb("b1_sb", [P, SLOTS * FK])
        b2_sb = sb("b2_sb", [P, SLOTS * D])
        gelu_warm = sb("gelu_warm", [P, 1])
        tile_token = sb("tile_token", [P, RING], I32)

        QTf = QT[:, :, :, :].rearrange("p a m t -> p (a m t)")
        KTf = KT[:, :, :, :, :, :].rearrange("p a m s r k -> p (a m s r k)")
        Vf = V[:, :, :, :].rearrange("p a m t -> p (a m t)")
        HALF = M8 * GT
        raw_q, raw_k = QTf[:, HALF:HALF + INNER], QTf[0:C, HALF + INNER:HALF + 2 * INNER]
        raw_v, raw_o = Vf[0:C, HALF:HALF + INNER], Vf[:, HALF + INNER:HALF + 2 * INNER]
        n2_T = [KTf[:, P * i:P * (i + 1)] for i in range(4)]
        hid_T = [KTf[:, 4 * P + F * i:4 * P + F * (i + 1)] for i in range(4)]
        w1_tile = [KTf[:, 4 * P + F * i:4 * P + F * (i + 1)] for i in range(4, 8)]
        half = [Vf, QTf]
        tile_rows = [half[i // (RING // 2)][:, ROW * (i % (RING // 2)):ROW * (i % (RING // 2) + 1)] for i in range(RING)]
        at = ROW * RING // 2
        tile_out = [half[i // (RING // 2)][:, at + D * (i % (RING // 2)):at + D * (i % (RING // 2) + 1)] for i in range(RING)]
        ysum = sb("ysum", [P, D])

        psJ = [psum("psJ0", [P, 512]), psum("psJ1", [P, 512])]
        psM = psum("psM", [P, 512])
        psT = psum("psT", [P, 512])
        psS = psum("psS", [P, 1024])
        psO = psum("psO", [P, 1024])

        s_small, s_ffn, s_bias = sem("s_small"), sem("s_ffn"), sem("s_bias")
        s_zeros = sem("s_zeros")
        s_raw = [sem(f"s_raw{i}") for i in range(4)]
        s_in = [sem("s_in0"), sem("s_in1")]
        s_res = [sem("s_res0"), sem("s_res1")]
        s_const, s_cc, s_tanh = sem("s_const"), sem("s_cc"), sem("s_tanh")
        s_wh, s_wl = sem("s_wh"), sem("s_wl")
        s_stat = sem("s_stat")
        s_agg = sem("s_agg")
        s_stat2, s_agg2 = sem("s_stat2"), sem("s_agg2")
        s_newton = sem("s_newton")
        s_zm, s_z = sem("s_zm"), sem("s_z")
        s_prep, s_xf = sem("s_prep"), sem("s_xf")
        s_hi, s_lo = sem("s_hi"), sem("s_lo")
        s_job, s_jobev = sem("s_job"), sem("s_jobev")
        s_qk, s_max, s_sub, s_exp = sem("s_qk"), sem("s_max"), sem("s_sub"), sem("s_exp")
        s_sum, s_inv, s_norm = sem("s_sum"), sem("s_inv"), sem("s_norm")
        s_pt, s_ptev = sem("s_pt"), sem("s_ptev")
        s_pv, s_oh, s_ol = sem("s_pv"), sem("s_oh"), sem("s_ol")
        s_oproj, s_aT = sem("s_oproj"), sem("s_aT")
        s_posta, s_x2 = sem("s_posta"), sem("s_x2")
        s_n2m, s_n2 = sem("s_n2m"), sem("s_n2")
        s_postb, s_n2T = sem("s_postb"), sem("s_n2T")
        s_logit, s_lmax, s_dl, s_el = sem("s_logit"), sem("s_lmax"), sem("s_dl"), sem("s_el")
        s_route = sem("s_route")
        s_hot = sem("s_hot")
        s_rank, s_ranked = sem("s_rank"), sem("s_ranked")
        s_place = sem("s_place")
        s_id, s_tok = sem("s_id"), sem("s_tok")
        s_scat = [sem("s_scat0"), sem("s_scat1")]
        s_pad, s_link = sem("s_pad"), sem("s_link")
        s_cols, s_tabT, s_tab = sem("s_cols"), sem("s_tabT"), sem("s_tab")
        s_row_tab = sem("s_row_tab")
        s_b1T, s_b1 = sem("s_b1T"), sem("s_b1")
        f_load = [sem(f"f_load{i}") for i in range(RING)]
        f_scat = [sem(f"f_scat{i}") for i in range(RING)]
        f_t1, f_t1ev, f_w1, f_gelu = sem("f_t1"), sem("f_t1ev"), sem("f_w1"), sem("f_gelu")
        f_pick = sem("f_pick")
        f_w2, f_sum, f_out = sem("f_w2"), sem("f_sum"), sem("f_out")
        f_send = sem("f_send")

        NEWT = 3 + 3 * NEWTON + 1
        N_SMALL = 7 * 16

        class Plan:

            def __init__(self, u, k, tail=False):
                self.k, self.j = k, k // 2
                self.odd = k % 2 == 1
                self.g = 2 * u + k // 2
                self.s = 4 * u + k
                self.u = u
                self.fixed = isinstance(u, int)

            def group(self, lag):
                g = self.g - lag
                if self.fixed and not 0 <= g < GROUPS:
                    return None
                return g

            def pair(self, lag):
                s = self.s - lag
                if self.fixed and not 0 <= s < PAIRS:
                    return None
                return s

            def par(self, lag=0):
                return (self.j - lag) % 2

            def uses(self, lag):
                return self.u + (self.j - lag - self.par(lag)) // 2 + 1

        STEPS_U = GROUPS // 2 + 2

        def run(eng, step):
            for u in range(LOOP_FROM):
                for k in range(4):
                    step(Plan(u, k))
            with eng.Fori(LOOP_FROM, LOOP_TO) as u:
                for k in range(4):
                    step(Plan(u, k))
            for u in range(LOOP_TO, STEPS_U):
                for k in range(4):
                    step(Plan(u, k))

        def entries(engine, tab, first, count, most):
            _, values = nc.values_load_multi_w_load_instructions(
                tab[0:1, bass.ds(first, count)], engines=[engine], min_val=0, max_val=most)
            return values

        def ffn_run(eng, engine, ffn):
            def experts(words, i):
                def expert(n):
                    at = PACK + i - n
                    return eng.snap((words[at // PACK] >> (4 * (at % PACK))) & (SLOTS - 1))
                return expert

            words = [None] + list(entries(engine, expert_tab, 0, RING // PACK, 2 ** 16 - 1))
            for t in range(RING):
                ffn(t, 0, t, [t - n >= 0 for n in range(5)], experts(words, t))
            with eng.Fori(1, TILES // RING) as v:
                words = entries(engine, expert_tab, v * (RING // PACK) - 1, RING // PACK + 1, 2 ** 16 - 1)
                for i in range(RING):
                    ffn(v * RING + i, v, i, [True] * 5, experts(words, i))
            words = entries(engine, expert_tab, TILES // PACK - 1, 1, 2 ** 16 - 1)
            for i in range(4):
                ffn(TILES + i, TILES // RING, i, [i - n < 0 for n in range(5)], experts(words, i))

        block = stack.enter_context(nc.Block())

        @block.sync
        def _(sp):
            def load_in(g, par, used):
                sp.dma_start(x_in[:, par, :, :], x_t[g]).then_inc(s_in[par], 16)
                sp.dma_start(c_in[:, par, :, :], c_t[g]).then_inc(s_in[par], 16)

            load_in(0, 0, 0)
            for i, (w, raw) in enumerate(((Wq, raw_q), (Wk, raw_k), (Wv, raw_v))):
                sp.dma_start(raw, w).then_inc(s_raw[i], 16)
                if i == 1:
                    load_in(1, 1, 0)
            sp.dma_start(raw_o.rearrange("p (m d) -> p m d", m=M8),
                         Wo.rearrange("(m p) d -> p m d", p=P)).then_inc(s_raw[3], 16)
            for g in (2, 3):
                sp.wait_ge(s_zm, 2 * (g - 1))
                load_in(g, g % 2, 1)
            sp.dma_start(w1_sb[:, 0:E * F].rearrange("d (e f) -> d e f", e=E),
                         w1.rearrange("e d f -> d e f")).then_inc(s_ffn, 16)
            sp.dma_start(w2_sb[:, 0:E * F].rearrange("p (e k d) -> p e k d", e=E, k=FK),
                         w2.rearrange("e (k p) d -> p e k d", p=P)).then_inc(s_ffn, 16)
            sp.dma_start(b1_rows[:, :], b1.rearrange("e (k p) -> (e k) p", p=P)).then_inc(s_bias, 16)
            sp.dma_start(b2_sb[:, 0:E * D], b2.rearrange("(a e) d -> a (e d)", a=1).to_broadcast([P, E * D])).then_inc(s_bias, 16)
            sp.wait_ge(s_cc, 3)
            sp.dma_start(rows_dram[0:E * REGION, :].rearrange("(e r) c -> r e c", e=E)[0:P],
                         pad_row[:, :].unsqueeze(1).to_broadcast([P, E, ROW])).then_inc(s_pad, 16)
            sp.dma_start(rows_dram[E * REGION:E * REGION + P, :], pad_row[:, :]).then_inc(s_pad, 16)

            def step(p):
                if p.odd:
                    return
                ahead, now = p.group(-4), p.group(0)
                a = sp.snap(ahead) if ahead is not None and not p.fixed else ahead
                b = sp.snap(now) if now is not None and not p.fixed else now
                if ahead is not None:
                    sp.wait_ge(s_zm, 2 * (p.g + 3))
                    load_in(a, p.par(), 0)
                if now is not None:
                    if not (p.fixed and p.g < 2):
                        sp.wait_ge(s_x2, p.g - 1)
                    sp.dma_start(x_res[:, p.par(), :, :], x_t[b]).then_inc(s_res[p.par()], 16)

            run(sp, step)

            for i in range(2):
                sp.wait_ge(s_scat[i], 32 * (GROUPS // 2))
            sp.wait_ge(s_pad, 32)
            sp.wait_ge(s_pv, PAIRS)
            sp.wait_ge(s_row_tab, 1)

            def load_rows(t, r, i, trips):
                if not (isinstance(t, int) and t < RING):
                    sp.wait_ge(f_out, t - RING + 1)
                sp.dma_start(tile_rows[i], rows_dram[bass.ds(r, P), :]).then_inc(f_load[i], 16)

            def load_trip(v):
                for i in range(RING):
                    if i % PACK == 0:
                        starts = entries(mybir.EngineType.SP, row_tab, v * RING + i, PACK, E * REGION)
                    load_rows(v * RING + i, starts[i % PACK], i, v)

            load_trip(0)
            with sp.Fori(1, TILES // RING) as v:
                load_trip(v)

        @block.gpsimd
        def _(pool):
            pool.memset(ident[:, :], 0.0).then_inc(s_const, 1)
            pool.memset(ones_b[:, :], 1.0).then_inc(s_const, 1)
            pool.memset(zero1[:, :], 0.0).then_inc(s_const, 1)
            pool.memset(pad_row[:, :], 0.0).then_inc(s_const, 1)
            pool.memset(one14[:, :], 1.0).then_inc(s_const, 1)
            pool.memset(mv[:, :, :], 1.0).then_inc(s_const, 1)
            pool.memset(var_mul[:, 0:2], 1.0 + EPS).then_inc(s_const, 1)
            pool.memset(var_mul[:, 2:6], 1.0).then_inc(s_const, 1)
            pool.memset(var_add[:, 0:2], EPS * EPS).then_inc(s_const, 1)
            pool.memset(var_add[:, 2:6], EPS).then_inc(s_const, 1)
            pool.iota(e_int[:, :, :], pattern=[[0, 2], [1, E]], base=0, channel_multiplier=0).then_inc(s_const, 1)
            pool.iota(r_int[:, :], pattern=[[REGION, E]], base=P, channel_multiplier=0).then_inc(s_const, 1)
            pool.iota(token[:, :], pattern=[[P, 2]], base=0, channel_multiplier=1).then_inc(s_const, 1)
            pool.iota(token_step[:, :], pattern=[[0, 2]], base=GT, channel_multiplier=0).then_inc(s_const, 1)
            pool.iota(t_int[:, 0:1], pattern=[[0, 1]], base=0, channel_multiplier=1).then_inc(s_const, 1)
            pool.iota(t_int[:, 1:2], pattern=[[0, 1]], base=-P, channel_multiplier=-P).then_inc(s_const, 1)
            pool.memset(move[:, :], 2.0 * E * REGION).then_inc(s_const, 1)
            pool.wait_ge(s_const, 17)
            pool.affine_select(out=ident[:, :], in_=ident[:, :], compare_op=ALU.not_equal, fill=1.0, base=0,
                               pattern=[[-1, P]], channel_multiplier=1).then_inc(s_cc, 1)
            pool.affine_select(out=before[:, :], in_=ones_b[:, :], compare_op=ALU.is_gt, fill=0.0, base=0,
                               pattern=[[1, P]], channel_multiplier=-1).then_inc(s_cc, 1)
            pool.iota(pad_row[:, ROW - 1:ROW].bitcast(I32), pattern=[[0, 1]], base=TOK,
                      channel_multiplier=0).then_inc(s_cc, 1)

            def norm_in(p):
                g = p.group(-2)
                if g is None:
                    return
                par = p.par()
                r_x, r_c = (rstd[:, a:a + 2].unsqueeze(2) for a in (0, 2))
                sh_x, sh_c = (shift[:, a:a + 2].unsqueeze(2) for a in (0, 2))
                pool.wait_ge(s_newton, NEWT * (p.g + 3))
                if not (p.fixed and p.g < -1):
                    pool.wait_ge(s_prep, p.g + 2)
                pool.tensor_tensor(zx[:, :, :], x_in[:, par, :, :], r_x.to_broadcast([P, 2, D]),
                                   ALU.mult).then_inc(s_zm, 1)
                pool.tensor_tensor(zc[:, :, :], c_in[:, par, :, :], r_c.to_broadcast([P, 2, C]),
                                   ALU.mult).then_inc(s_zm, 1)
                pool.wait_ge(s_zm, 2 * (p.g + 3))
                pool.tensor_tensor(zx[:, :, :], zx[:, :, :], sh_x.to_broadcast([P, 2, D]), ALU.add).then_inc(s_z, 1)
                pool.tensor_tensor(zc[:, :, :], zc[:, :, :], sh_c.to_broadcast([P, 2, C]), ALU.add).then_inc(s_z, 1)

            def norm_x2(p):
                g = p.group(2)
                if g is None:
                    return
                par = p.par()
                n2 = rows[:, par, :, D:2 * D]
                pool.wait_ge(s_newton, NEWT * (p.g + 3))
                pool.tensor_tensor(n2, rows[:, par, :, 0:D], rstd[:, 4:6].unsqueeze(2).to_broadcast([P, 2, D]),
                                   ALU.mult).then_inc(s_n2m, 1)
                pool.wait_ge(s_n2m, p.g - 1)
                pool.tensor_tensor(n2, n2, shift[:, 4:6].unsqueeze(2).to_broadcast([P, 2, D]),
                                   ALU.add).then_inc(s_n2, 1)

            def split_in(p):
                g = p.group(-2)
                if g is None:
                    return
                par = p.par()
                pool.wait_ge(s_xf, 2 * (p.g + 3))
                if not (p.fixed and p.g < 0):
                    pool.wait_ge(s_job, 12 * (p.g + 1))
                pool.tensor_tensor(XT_h[:, par, :], xf[:, :], zero1[:, :].to_broadcast([P, GT]), ALU.add).then_inc(s_hi, 1)
                pool.tensor_tensor(CT_h[:, par, :], cf[:, :], zero1[0:C, :].to_broadcast([C, GT]), ALU.add).then_inc(s_hi, 1)
                pool.wait_ge(s_hi, 2 * (p.g + 3))
                pool.tensor_tensor(XT_l[:, par, :], xf[:, :], XT_h[:, par, :], ALU.subtract).then_inc(s_lo, 1)
                pool.tensor_tensor(CT_l[:, par, :], cf[:, :], CT_h[:, par, :], ALU.subtract).then_inc(s_lo, 1)

            def send(p):
                g = p.group(3)
                if g is None:
                    return
                par = p.par(3)
                pool.wait_ge(s_route, 6 * (p.g - 2))
                if not (p.fixed and p.g < 4):
                    pool.wait_ge(s_tok, p.g - 3)
                pool.tensor_tensor(rows[:, par, :, ROW - 1].bitcast(I32), token[:, :],
                                   zero1[:, :].bitcast(I32).to_broadcast([P, 2]), ALU.add).then_inc(s_id, 1)
                pool.wait_ge(s_place, 3 * (p.g - 2))
                pool.wait_ge(s_id, p.g - 2)
                pool.tensor_tensor(token[:, :], token[:, :], token_step[:, :], ALU.add).then_inc(s_tok, 1)
                for t in range(2):
                    pool.indirect_dma_start(rows_dram, bass.IndirectOffsetOnAxis(place_i[:, par, t:t + 1], 0),
                                            rows[:, par, t, :], None).then_inc(s_scat[par], 16)

            def step(p):
                if p.odd:
                    split_in(p)
                    send(p)
                else:
                    norm_in(p)
                    norm_x2(p)

            norm_in(Plan(-1, 0))
            split_in(Plan(-1, 0))
            norm_in(Plan(-1, 2))
            pool.wait_ge(s_z, 4)
            for r in range(2):
                pool.memset(KT[64 * r:64 * r + 64, :, :, :, 1 - r, :].rearrange("p a m s k -> p (a m s) k"), 0.0).then_inc(s_zeros, 1)
                pool.wait_ge(s_zeros, r + 1)
            split_in(Plan(-1, 2))
            pool.wait_ge(s_lo, 4)
            for b in range(2):
                pool.memset(PTs[64 * b:64 * b + 64, :, :, :, 1 - b, :].rearrange("p a h m q -> p (a h m) q"), 0.0).then_inc(s_zeros, 1)
                pool.wait_ge(s_zeros, b + 3)
            run(pool, step)

            def send_out(t, i, trips):
                pool.wait_ge(f_out, t + 1)
                pool.sem_inc(f_send, 1)
                pool.indirect_dma_start(out_rows, bass.IndirectOffsetOnAxis(tile_token[:, i:i + 1], 0),
                                        tile_out[i], None, bounds_check=TOK - 1, oob_is_err=False).then_inc(f_scat[i], 16)

            with pool.Fori(0, TILES // RING) as v:
                for i in range(RING):
                    send_out(v * RING + i, i, v)
            for i in range(RING):
                pool.wait_ge(f_scat[i], 16 * (TILES // RING))

        @block.scalar
        def _(act):
            small = ((gx_col[:, :], g_x.rearrange("(p a) -> p a", a=1)), (bx_col[:, :], b_x.rearrange("(p a) -> p a", a=1)),
                     (gc_col[:, :], g_c.rearrange("(p a) -> p a", a=1)), (bc_col[:, :], b_c.rearrange("(p a) -> p a", a=1)),
                     (gates[:, 0:1], g_xattn.rearrange("(p a) -> p a", a=1).to_broadcast([P, 1])),
                     (gates[:, 1:2], g_ffn.rearrange("(p a) -> p a", a=1).to_broadcast([P, 1])),
                     (rw_sb[:, :], router_w))
            for dst, src in small:
                act.dma_start(dst, src).then_inc(s_small, 16)
            def weight_high(i, dst, raw):
                act.activation(dst, raw, ACT.Copy).then_inc(s_wh, 1)

            def job(p, n):
                if p.group(-1) is None:
                    return
                par = p.par(-1)
                act.wait_ge(s_job, 12 * (p.g + 1) + n + 1)
                if n < 4:
                    dst = QT[:, par, 2 * n:2 * n + 2, :].rearrange("p m t -> p (m t)")
                elif n == 4 or 7 <= n <= 9:
                    m = 0 if n == 4 else n - 6
                    for r in range(2):
                        part = slice(64 * r, 64 * r + 64)
                        last = act.activation(KT[part, par, 2 * m:2 * m + 2, :, r, :].rearrange("p m s k -> p (m s) k"),
                                              psJ[n % 2][part, :].rearrange("p (n k) -> p n k", k=SEQ), ACT.Copy)
                    last.then_inc(s_jobev, 1)
                    return
                else:
                    pr, half = (0, n - 5) if n < 7 else (1, n - 10)
                    dst = V[:, par, pr, 512 * half:512 * half + 512]
                act.activation(dst, psJ[n % 2][:, :], ACT.Copy).then_inc(s_jobev, 1)

            def values_high(p):
                s = p.pair(2)
                if s is None:
                    return
                act.wait_ge(s_pv, p.s - 1)
                dst = OT_h[:, :, (p.k % 2) * P:(p.k % 2 + 1) * P]
                act.activation(dst, psO[:, :].rearrange("p (m t) -> p m t", m=M8), ACT.Copy).then_inc(s_oh, 1)

            def probs_out(p, half):
                if p.pair(1) is None:
                    return
                if p.fixed and p.s == 1:
                    act.wait_ge(s_zeros, 4)
                act.wait_ge(s_pt, 2 * (p.s - 1) + half + 1)
                for b in range(2):
                    part = slice(64 * b, 64 * b + 64)
                    act.activation(PTs[part, (p.k - 1) % 2, half, :, b, :], psT[part, :].rearrange("p (m q) -> p m q", m=M8),
                                   ACT.Copy).then_inc(s_ptev, 1)

            def expo(p):
                if p.pair(0) is None:
                    return
                act.wait_ge(s_sub, p.s + 1)
                act.activation(probs[:, p.k % 2, :, :], probs[:, p.k % 2, :, :], ACT.Exp, scale=SCALE).then_inc(s_exp, 1)

            def attn_out(p):
                if p.group(1) is None:
                    return
                act.wait_ge(s_oproj, p.g)
                act.activation(aT[:, :], psM[:, 0:GT], ACT.Copy, scale=tanhs[:, 0:1]).then_inc(s_aT, 1)

            def norm_T(p):
                if p.group(2) is None:
                    return
                act.wait_ge(s_postb, p.g - 1)
                act.activation(n2T[:, :], psM[:, 0:GT], ACT.Copy).then_inc(s_n2T, 1)

            def route_exp(p):
                if p.group(3) is None:
                    return
                act.wait_ge(s_dl, p.g - 2)
                act.activation(el[:, :, :], dl[:, :, :], ACT.Exp).then_inc(s_el, 1)

            def step(p):
                if p.odd:
                    job(p, 7)
                    job(p, 8)
                    probs_out(p, 0)
                    job(p, 9)
                    values_high(p)
                    norm_T(p)
                    expo(p)
                    job(p, 10)
                    probs_out(p, 1)
                    job(p, 11)
                    attn_out(p)
                else:
                    job(p, 0)
                    job(p, 1)
                    route_exp(p)
                    probs_out(p, 0)
                    job(p, 2)
                    expo(p)
                    job(p, 3)
                    job(p, 4)
                    job(p, 5)
                    values_high(p)
                    probs_out(p, 1)
                    job(p, 6)

            for i, (dst, raw) in enumerate(((Wq_h[:, :], raw_q), (Wk_h[:, :], raw_k), (Wv_h[:, :], raw_v),
                                            (Wo_h[:, :, :].rearrange("p m d -> p (m d)"), raw_o))):
                act.wait_ge(s_raw[i], 16)
                weight_high(i, dst, raw)
            for n in range(12):
                job(Plan(-1, 2), n)
            act.wait_ge(s_small, N_SMALL)
            act.activation(tanhs[:, :], gates[:, :], ACT.Tanh).then_inc(s_tanh, 1)
            run(act, step)

            def ffn(t, v, i, on, expert):
                if on[2]:
                    e = expert(2)
                    at = [act.snap(e * FK + k) for k in range(FK)]
                if on[0]:
                    act.wait_ge(f_t1, t + 1)
                    act.activation(n2_T[i % 4], psJ[i % 2][:, 0:P], ACT.Copy).then_inc(f_t1ev, 1)
                if on[2]:
                    act.wait_ge(f_w1, t - 1)
                    if not (isinstance(t, int) and t < 6):
                        act.wait_ge(f_w2, t - 5)
                    for k in range(FK):
                        act.activation(hid_T[(i - 2) % 4][:, P * k:P * k + P], (psM, psT)[i % 2][:, P * k:P * k + P], ACT.Gelu,
                                       bias=b1_sb[:, bass.ds(at[k], 1)]).then_inc(f_gelu, 1)

            act.activation(gelu_warm[:, :], zero1[:, :], ACT.Gelu)
            act.wait_ge(s_b1T, 1)
            act.activation(b1_sb[:, 0:E * FK], psT[:, 0:E * FK], ACT.Copy).then_inc(s_b1, 1)
            act.wait_ge(s_b1, 1)
            act.wait_ge(s_tab, 1)
            ffn_run(act, mybir.EngineType.Activation, ffn)

        @block.tensor
        def _(pe):
            misc = [None]

            def misc_free():
                if misc[0] is not None:
                    pe.wait_ge(*misc[0])

            def split3(outs, w_h, w_l, r_h, r_l):
                return [lambda: pe.matmul(outs, w_h, r_h, start=True, stop=False),
                        lambda: pe.matmul(outs, w_h, r_l, start=False, stop=False),
                        lambda: pe.matmul(outs, w_l, r_h, start=False, stop=True)]

            def prep(p):
                if p.group(-2) is None:
                    return
                misc_free()
                pe.wait_ge(s_z, 2 * (p.g + 3))
                for t in range(2):
                    pe.transpose(psM[:, P * t:P * t + P], zx[:, t, :], ident[:, :])
                for t in range(2):
                    last = pe.transpose(psM[0:C, GT + P * t:GT + P * t + P], zc[:, t, :], ident[:, :])
                last.then_inc(s_prep, 1)
                misc[0] = (s_xf, 2 * (p.g + 3))

            def job(p, n, half=None, ahead=None):
                if p.group(-1) is None:
                    if ahead:
                        ahead()
                    return
                par = p.par(-1)
                bank = psJ[n % 2]
                if half != 1:
                    if n == 0:
                        pe.wait_ge(s_lo, 2 * (p.g + 2))
                    if not (p.fixed and 12 * (p.g + 1) + n < 2):
                        pe.wait_ge(s_jobev, 12 * (p.g + 1) + n - 1)
                if n < 5 or 7 <= n <= 9:
                    w_h, w_l, r_h, r_l = (Wq_h, Wq_l, XT_h, XT_l) if n < 4 else (Wk_h, Wk_l, CT_h, CT_l)
                    m0 = 2 * n if n < 4 else 0 if n == 4 else 2 * (n - 6)
                    products = []
                    for i in range(2):
                        cols = slice((m0 + i) * P, (m0 + i + 1) * P)
                        products += split3(bank[:, GT * i:GT * i + GT], w_h[:, cols], w_l[:, cols], r_h[:, par, :], r_l[:, par, :])
                    middle = 3
                else:
                    pr, h = (0, n - 5) if n < 7 else (1, n - 10)
                    tok, cols = slice(pr * P, pr * P + P), slice(512 * h, 512 * h + 512)
                    products = split3(bank[:, :], CT_h[:, par, tok], CT_l[:, par, tok], Wv_h[:, cols], Wv_l[:, cols])
                    middle = 2
                products = {None: products, 0: products[:middle], 1: products[middle:]}[half]
                for product in products[:-1]:
                    product()
                if ahead:
                    ahead()
                last = products[-1]()
                if half != 0:
                    last.then_inc(s_job, 1)

            def scores(p, part_of_4):
                if p.pair(0) is None:
                    return
                for g in range(HG // 4 * part_of_4, HG // 4 * (part_of_4 + 1)):
                    for b in range(2):
                        for c in range(2):
                            m, seq = 2 * g + c, 2 * (p.k % 2) + b
                            col = (2 * g + b) * 2 * SEQ
                            last = pe.matmul(psS[64 * c:64 * c + 64, col:col + 2 * SEQ],
                                             QT[:, p.par(), m, SEQ * seq:SEQ * seq + SEQ],
                                             KT[:, p.par(), m, seq, :, :].rearrange("p r k -> p (r k)"),
                                             start=True, stop=True)
                if part_of_4 == 3:
                    last.then_inc(s_qk, 1)

            def value_sums(p, part_of_4):
                if p.pair(2) is None:
                    return
                for m in range(M8 // 4 * part_of_4, M8 // 4 * (part_of_4 + 1)):
                    for h in range(2):
                        head = 2 * m + h
                        last = pe.matmul(psO[64 * h:64 * h + 64, m * P:(m + 1) * P],
                                         V[:, p.par(1), p.k % 2, head * DH:head * DH + DH],
                                         PTs[:, p.k % 2, h, m, :, :].rearrange("p b q -> p (b q)"),
                                         start=True, stop=True)
                if part_of_4 == 3:
                    last.then_inc(s_pv, 1)

            def scores_ready(p):
                s = p.s + 1
                if p.fixed and s >= PAIRS:
                    return
                if not (p.fixed and s < 1):
                    pe.wait_ge(s_sub, s)
                if p.odd:
                    pe.wait_ge(s_jobev, 12 * (p.g + 1) + 10)

            def sums_ready(p):
                if p.pair(2) is None:
                    return
                pe.wait_ge(s_ptev, 4 * (p.s - 1))
                if not (p.fixed and p.s < 3):
                    pe.wait_ge(s_ol, p.s - 2)

            def probs_T(p, half):
                if p.pair(1) is None:
                    return
                if half == 0:
                    pe.wait_ge(s_norm, p.s)
                if not (p.fixed and 2 * (p.s - 1) + half < 1):
                    pe.wait_ge(s_ptev, 4 * (p.s - 1) + 2 * half)
                for g in range(HG):
                    src = probs[:, (p.k - 1) % 2, 8 * half + 2 * g:8 * half + 2 * g + 2, :].rearrange("p b k -> p (b k)")
                    last = pe.transpose(psT[:, P * g:P * g + P], src, ident[:, :])
                last.then_inc(s_pt, 1)

            def out_proj(p, ahead):
                if p.group(1) is None:
                    ahead()
                    return
                misc_free()
                pe.wait_ge(s_oh, 2 * p.g)
                for m in range(M8):
                    pe.matmul(psM[:, 0:GT], Wo_h[:, m, :], OT_h[:, m, :], start=(m == 0), stop=False)
                    pe.matmul(psM[:, 0:GT], Wo_l[:, m, :], OT_h[:, m, :], start=False, stop=False)
                pe.wait_ge(s_ol, 2 * p.g)
                for m in range(M8):
                    if m == M8 - 1:
                        ahead()
                    last = pe.matmul(psM[:, 0:GT], Wo_h[:, m, :], OT_l[:, m, :], start=False, stop=(m == M8 - 1))
                last.then_inc(s_oproj, 1)
                misc[0] = (s_aT, p.g)

            def post_a(p):
                if p.group(2) is None:
                    return
                misc_free()
                pe.wait_ge(s_aT, p.g - 1)
                for t in range(2):
                    last = pe.transpose(psM[:, P * t:P * t + P], aT[:, P * t:P * t + P], ident[:, :])
                last.then_inc(s_posta, 1)
                misc[0] = (s_x2, p.g - 1)

            def post_b(p):
                if p.group(2) is None:
                    return
                misc_free()
                pe.wait_ge(s_n2, p.g - 1)
                for t in range(2):
                    last = pe.transpose(psM[:, P * t:P * t + P], rows[:, p.par(), t, D:2 * D], ident[:, :])
                last.then_inc(s_postb, 1)
                misc[0] = (s_n2T, p.g - 1)

            def router(p):
                if p.group(3) is None:
                    return
                misc_free()
                pe.wait_ge(s_n2T, p.g - 2)
                for t in range(2):
                    last = pe.matmul(psM[:, E * t:E * t + E], n2T[:, P * t:P * t + P], rw_sb[:, :], start=True, stop=True)
                last.then_inc(s_logit, 1)
                misc[0] = (s_dl, p.g - 2)

            def rank(p):
                if p.group(3) is None:
                    return
                misc_free()
                pe.wait_ge(s_hot, p.g - 2)
                pe.matmul(psM[:, 0:E], before[:, :], onehot[:, 0, :], start=True, stop=True)
                pe.matmul(psM[:, E:2 * E], ones_b[:, :], onehot[:, 0, :], start=True, stop=False)
                pe.matmul(psM[:, E:2 * E], before[:, :], onehot[:, 1, :], start=False, stop=True)
                pe.matmul(psM[:, 2 * E:3 * E], ones_b[:, :], onehot[:, 0, :], start=True, stop=False)
                pe.matmul(psM[:, 2 * E:3 * E], ones_b[:, :], onehot[:, 1, :], start=False, stop=True).then_inc(s_rank, 1)
                misc[0] = (s_ranked, p.g - 2)

            def step(p):
                if p.k == 0:
                    misc[0] = (s_aT, p.g - 1) if p.group(2) is not None else misc[0]
                if p.odd:
                    scores(p, 0)
                    job(p, 7, 0)
                    scores(p, 1)
                    job(p, 7, 1)
                    scores(p, 2)
                    job(p, 8, 0)
                    scores(p, 3)
                    job(p, 8, 1, lambda: sums_ready(p))
                    value_sums(p, 0)
                    job(p, 9, 0)
                    probs_T(p, 0)
                    value_sums(p, 1)
                    prep(p)
                    job(p, 9, 1)
                    value_sums(p, 2)
                    job(p, 10, 0)
                    value_sums(p, 3)
                    job(p, 10, 1)
                    post_b(p)
                    job(p, 11, 0)
                    probs_T(p, 1)
                    job(p, 11, 1)
                    out_proj(p, lambda: scores_ready(p))
                else:
                    scores(p, 0)
                    job(p, 0, 0)
                    scores(p, 1)
                    job(p, 0, 1)
                    router(p)
                    scores(p, 2)
                    job(p, 1, 0)
                    probs_T(p, 0)
                    scores(p, 3)
                    job(p, 1, 1, lambda: sums_ready(p))
                    value_sums(p, 0)
                    job(p, 2, 0)
                    post_a(p)
                    value_sums(p, 1)
                    job(p, 2, 1)
                    value_sums(p, 2)
                    job(p, 3, 0)
                    value_sums(p, 3)
                    job(p, 3, 1)
                    job(p, 4)
                    probs_T(p, 1)
                    job(p, 5, 0)
                    rank(p)
                    job(p, 5, 1)
                    job(p, 6, ahead=lambda: scores_ready(p))

            pe.wait_ge(s_cc, 2)
            prep(Plan(-1, 0))
            for n in range(12):
                if n in (0, 4, 5):
                    pe.wait_ge(s_wl, (0, 4, 5).index(n) + 1)
                if n == 6:
                    prep(Plan(-1, 2))
                job(Plan(-1, 2), n)
            pe.wait_ge(s_wl, 4)
            pe.wait_ge(s_zeros, 2)
            pe.wait_ge(s_jobev, 10)
            run(pe, step)

            def ffn(t, v, i, on, expert):
                if on[4]:
                    e = expert(4)
                    at = [pe.snap(e * F + k * D) for k in range(FK)]
                if on[0]:
                    if not (isinstance(t, int) and t < 2):
                        pe.wait_ge(f_t1ev, t - 1)
                    pe.wait_ge(f_load[i], 16 * (v + 1))
                    pe.transpose(psJ[i % 2][:, 0:P], tile_rows[i][:, D:2 * D], ident[:, :]).then_inc(f_t1, 1)
                if on[2]:
                    pe.wait_ge(f_t1ev, t - 1)
                    pe.wait_ge(f_pick, t - 1)
                    if not (isinstance(t, int) and t < 4):
                        pe.wait_ge(f_gelu, FK * (t - 3))
                    for k in range(FK):
                        last = pe.matmul((psM, psT)[i % 2][:, P * k:P * k + P], w1_tile[(i - 2) % 4][:, P * k:P * k + P],
                                         n2_T[(i - 2) % 4], start=True, stop=True)
                    last.then_inc(f_w1, 1)
                if on[4]:
                    o = 512 * (i % 2)
                    pe.wait_ge(f_gelu, FK * (t - 3))
                    if not (isinstance(t, int) and t < 6):
                        pe.wait_ge(f_sum, t - 5)
                    for k in range(FK):
                        last = pe.matmul(psO[:, o:o + D], hid_T[i % 4][:, P * k:P * k + P],
                                         w2_sb[:, bass.ds(at[k], D)], start=(k == 0), stop=(k == FK - 1))
                    last.then_inc(f_w2, 1)

            pe.wait_ge(s_bias, 32)
            pe.wait_ge(s_ptev, 4 * PAIRS)
            pe.transpose(psT[:, 0:E * FK], b1_rows[:, :], ident[0:E * FK, 0:E * FK]).then_inc(s_b1T, 1)
            pe.wait_ge(s_cols, 3)
            for i in range(2):
                last = pe.transpose(psM[0:1, P * i:P * i + P], t_cols[:, i:i + 1], ident[:, :])
            last.then_inc(s_tabT, 1)
            pe.wait_ge(s_ffn, 32)
            pe.wait_ge(s_b1, 1)
            pe.wait_ge(s_tab, 1)
            ffn_run(pe, mybir.EngineType.PE, ffn)

        @block.vector
        def _(dve):
            def stats_in(p):
                if p.group(-2) is None:
                    return
                par = p.par()
                dve.wait_ge(s_in[par], 32 * p.uses(-2))
                if not (p.fixed and p.g < -1):
                    dve.wait_ge(s_agg, 4 * (p.g + 2))
                for t in range(2):
                    dve.bn_stats(bn6[:, t, :], x_in[:, par, t, :]).then_inc(s_stat, 1)
                for t in range(2):
                    dve.bn_stats(bn6[:, 2 + t, :], c_in[:, par, t, :]).then_inc(s_stat, 1)

            def stats_in_done(p):
                if p.group(-2) is not None:
                    dve.wait_ge(s_stat, 4 * (p.g + 3))
                    if not (p.fixed and p.g < -1):
                        dve.wait_ge(s_newton, NEWT * (p.g + 2))

            def means_in(p):
                if p.group(-2) is None:
                    return
                for t in range(4):
                    dve.bn_aggr(mv[:, t, :], bn6[:, t, :]).then_inc(s_agg, 1)

            def roots(p):
                if p.group(-2) is None and p.group(2) is None:
                    return
                n = NEWT * (p.g + 2)
                if p.group(-2) is not None:
                    dve.wait_ge(s_agg, 4 * (p.g + 3))
                if p.group(2) is not None:
                    dve.wait_ge(s_agg2, 2 * (p.g - 1))
                dve.tensor_tensor(nw[:, :], mv[:, :, 1], var_mul[:, :], ALU.mult).then_inc(s_newton, 1)
                dve.wait_ge(s_newton, n + 1)
                dve.tensor_tensor(nw[:, :], nw[:, :], var_add[:, :], ALU.add).then_inc(s_newton, 1)
                dve.wait_ge(s_newton, n + 2)
                if not (p.fixed and p.g < -1):
                    if not (p.fixed and p.g + 1 >= GROUPS):
                        dve.wait_ge(s_z, 2 * (p.g + 2))
                if not (p.fixed and not 0 <= p.g - 3 < GROUPS):
                    dve.wait_ge(s_n2, p.g - 2)
                dve.tensor_scalar(rstd[:, :].bitcast(I32), nw[:, :].bitcast(I32), -0.5, RSQRT_SEED,
                                  ALU.mult, ALU.add).then_inc(s_newton, 1)
                n += 3
                for _ in range(NEWTON):
                    dve.wait_ge(s_newton, n)
                    dve.tensor_tensor(nq[:, :], rstd[:, :], rstd[:, :], ALU.mult).then_inc(s_newton, 1)
                    dve.wait_ge(s_newton, n + 1)
                    dve.scalar_tensor_tensor(nq[:, :], nq[:, :], -0.5, nw[:, :], ALU.mult, ALU.mult).then_inc(s_newton, 1)
                    dve.wait_ge(s_newton, n + 2)
                    dve.scalar_tensor_tensor(rstd[:, :], nq[:, :], 1.5, rstd[:, :], ALU.add, ALU.mult).then_inc(s_newton, 1)
                    n += 3
                dve.wait_ge(s_newton, n)
                dve.scalar_tensor_tensor(shift[:, :], mv[:, :, 0], -1.0, rstd[:, :], ALU.mult, ALU.mult).then_inc(s_newton, 1)

            def prep(p):
                if p.group(-2) is None:
                    return
                dve.wait_ge(s_prep, p.g + 3)
                if not (p.fixed and p.g < -1):
                    dve.wait_ge(s_lo, 2 * (p.g + 2))
                dve.tensor_scalar(xf[:, :], psM[:, 0:GT], gx_col[:, :], bx_col[:, :], ALU.mult, ALU.add).then_inc(s_xf, 1)
                dve.tensor_scalar(cf[:, :], psM[0:C, GT:2 * GT], gc_col[:, :], bc_col[:, :], ALU.mult,
                                  ALU.add).then_inc(s_xf, 1)

            def scores_max(p):
                if p.pair(0) is None:
                    return
                dve.wait_ge(s_qk, p.s + 1)
                dve.tensor_reduce(row_max[:, :], psS[:, :].rearrange("p (n k) -> p n k", k=SEQ), AX.X,
                                  ALU.max).then_inc(s_max, 1)

            def scores_sub(p):
                if p.pair(0) is None:
                    return
                dve.wait_ge(s_max, p.s + 1)
                dve.tensor_tensor(probs[:, p.k % 2, :, :].rearrange("p (r n) k -> p n r k", r=2),
                                  psS[:, :].rearrange("p (n r k) -> p n r k", r=2, k=SEQ),
                                  row_max[:, :].rearrange("p (n r) -> p n r", r=2).unsqueeze(3).to_broadcast([P, 8, 2, SEQ]),
                                  ALU.subtract).then_inc(s_sub, 1)

            def sums(p):
                if p.pair(0) is None:
                    return
                pr = probs[:, p.k % 2, :, :]
                dve.wait_ge(s_exp, p.s + 1)
                dve.tensor_reduce(row_sum[:, :], pr, AX.X, ALU.add).then_inc(s_sum, 1)
                dve.wait_ge(s_sum, p.s + 1)
                dve.reciprocal(row_inv[:, :], row_sum[:, :]).then_inc(s_inv, 1)

            def normalise(p):
                if p.pair(0) is None:
                    return
                pr = probs[:, p.k % 2, :, :]
                dve.wait_ge(s_inv, p.s + 1)
                dve.tensor_tensor(pr, pr, row_inv[:, :].unsqueeze(2).to_broadcast([P, 16, SEQ]), ALU.mult).then_inc(s_norm, 1)

            def values_low(p):
                if p.pair(2) is None:
                    return
                cols = slice((p.k % 2) * P, (p.k % 2 + 1) * P)
                dve.wait_ge(s_oh, p.s - 1)
                dve.tensor_tensor(OT_l[:, :, cols], psO[:, :].rearrange("p (m t) -> p m t", m=M8), OT_h[:, :, cols],
                                  ALU.subtract).then_inc(s_ol, 1)

            def residual(p):
                if p.group(2) is None:
                    return
                par = p.par()
                dve.wait_ge(s_res[par], 16 * p.uses(2))
                if not (p.fixed and p.g < 4):
                    dve.wait_ge(s_scat[par], 32 * p.uses(4))
                    dve.wait_ge(s_agg2, 2 * (p.g - 2))
                dve.wait_ge(s_posta, p.g - 1)
                dve.tensor_tensor(rows[:, par, :, 0:D], psM[:, 0:GT].rearrange("p (t d) -> p t d", t=2),
                                  x_res[:, par, :, :], ALU.add).then_inc(s_x2, 1)
                dve.wait_ge(s_x2, p.g - 1)
                for t in range(2):
                    dve.bn_stats(bn6[:, 4 + t, :], rows[:, par, t, 0:D]).then_inc(s_stat2, 1)

            def residual_done(p):
                if p.group(2) is not None:
                    dve.wait_ge(s_stat2, 2 * (p.g - 1))

            def means_x2(p):
                if p.group(2) is None:
                    return
                for t in range(2):
                    dve.bn_aggr(mv[:, 4 + t, :], bn6[:, 4 + t, :]).then_inc(s_agg2, 1)

            def route(p):
                if p.group(3) is None:
                    return
                n, par = 6 * (p.g - 3), p.par(3)
                logits = psM[:, 0:2 * E].rearrange("p (t e) -> p t e", t=2)
                dve.wait_ge(s_logit, p.g - 2)
                dve.tensor_reduce(lmax[:, :], logits, AX.X, ALU.max).then_inc(s_lmax, 1)
                dve.wait_ge(s_lmax, p.g - 2)
                dve.tensor_tensor(dl[:, :, :], logits, lmax[:, :].unsqueeze(2).to_broadcast([P, 2, E]),
                                  ALU.subtract).then_inc(s_dl, 1)
                dve.wait_ge(s_dl, p.g - 2)
                dve.tensor_scalar(cand[:, :, :], dl[:, :, :], 0.0, 2.0 * E, ALU.is_lt, ALU.mult).then_inc(s_route, 1)
                dve.wait_ge(s_route, n + 1)
                dve.tensor_tensor(cand[:, :, :], cand[:, :, :], e_iota[:, :, :], ALU.add).then_inc(s_route, 1)
                dve.wait_ge(s_route, n + 2)
                dve.tensor_reduce(first[:, :], cand[:, :, :], AX.X, ALU.min).then_inc(s_route, 1)
                dve.wait_ge(s_route, n + 3)
                dve.tensor_tensor(onehot[:, :, :], e_iota[:, :, :], first[:, :].unsqueeze(2).to_broadcast([P, 2, E]),
                                  ALU.is_equal).then_inc(s_hot, 1)

            def weight(p):
                if p.group(3) is None:
                    return
                n, par = 6 * (p.g - 3), p.par(3)
                dve.wait_ge(s_el, p.g - 2)
                dve.tensor_reduce(den[:, :], el[:, :, :], AX.X, ALU.add).then_inc(s_route, 1)
                dve.wait_ge(s_route, n + 4)
                dve.reciprocal(inv[:, :], den[:, :]).then_inc(s_route, 1)
                dve.wait_ge(s_route, n + 5)
                dve.tensor_scalar(rows[:, par, :, 2 * D], inv[:, :], tanhs[:, 1:2], None, ALU.mult).then_inc(s_route, 1)

            def places(p):
                if p.group(3) is None:
                    return
                n, par = 3 * (p.g - 3), p.par(3)
                dve.wait_ge(s_rank, p.g - 2)
                if not (p.fixed and p.g < 4):
                    dve.wait_ge(s_ranked, p.g - 3)
                dve.tensor_tensor(place[:, :, :], psM[:, 0:2 * E].rearrange("p (t e) -> p t e", t=2),
                                  next_row[:, :].unsqueeze(1).to_broadcast([P, 2, E]), ALU.add).then_inc(s_place, 1)
                dve.wait_ge(s_place, n + 1)
                dve.tensor_tensor(next_row[:, :], next_row[:, :], psM[:, 2 * E:3 * E], ALU.add).then_inc(s_ranked, 1)
                dve.tensor_tensor(place[:, :, :], place[:, :, :], onehot[:, :, :], ALU.mult).then_inc(s_place, 1)
                dve.wait_ge(s_place, n + 2)
                with nc.allow_low_precision(reason="whole numbers below 2**24"):
                    dve.tensor_reduce(place_i[:, par, :], place[:, :, :], AX.X, ALU.add).then_inc(s_place, 1)

            def step(p):
                if p.odd:
                    scores_max(p)
                    scores_sub(p)
                    prep(p)
                    weight(p)
                    values_low(p)
                    sums(p)
                    normalise(p)
                else:
                    stats_in(p)
                    route(p)
                    scores_max(p)
                    stats_in_done(p)
                    scores_sub(p)
                    means_in(p)
                    residual(p)
                    residual_done(p)
                    sums(p)
                    means_x2(p)
                    roots(p)
                    values_low(p)
                    normalise(p)
                    places(p)

            dve.wait_ge(s_const, 17)
            dve.tensor_copy(e_iota[:, :, :], e_int[:, :, :])
            dve.tensor_copy(next_row[:, :], r_int[:, :])
            dve.tensor_copy(t_f[:, :], t_int[:, :]).then_inc(s_link, 1)

            lows = ((Wq_l[:, :], Wq_h[:, :], raw_q), (Wk_l[:, :], Wk_h[:, :], raw_k), (Wv_l[:, :], Wv_h[:, :], raw_v),
                    (Wo_l[:, :, :].rearrange("p m d -> p (m d)"), Wo_h[:, :, :].rearrange("p m d -> p (m d)"), raw_o))
            for g in (-2, -1):
                q = Plan(-1, 2 * (g + 2))
                stats_in(q)
                stats_in_done(q)
                means_in(q)
                roots(q)
                for i in (0, 1) if g == -2 else (2, 3):
                    lo, hi, raw = lows[i]
                    dve.wait_ge(s_wh, i + 1)
                    dve.tensor_tensor(lo, raw, hi, ALU.subtract).then_inc(s_wl, 1)
                if g == -2:
                    dve.wait_ge(s_small, N_SMALL)
                prep(q)
            dve.wait_ge(s_tanh, 1)
            dve.wait_ge(s_link, 1)
            run(dve, step)

            def link(ins, n):
                ins.then_inc(s_link, 1)
                dve.wait_ge(s_link, n)

            dve.wait_ge(s_ranked, GROUPS)
            link(dve.tensor_tensor(n_tiles[:, :], next_row[:, :], r_int[:, :], ALU.subtract), 2)
            link(dve.tensor_scalar(ends_i[:, :], n_tiles[:, :], float(P - 1), None, ALU.add), 3)
            link(dve.tensor_scalar(ends_i[:, :], ends_i[:, :], 7, None, ALU.logical_shift_right), 4)
            link(dve.tensor_copy(n_tiles[:, :], ends_i[:, :]), 5)
            dve.tensor_tensor_scan(cum[:, :], one14[:, :], n_tiles[:, :], 0.0, ALU.mult, ALU.add).then_inc(s_link, 1)
            dve.tensor_tensor(move[:, 0:E - 1], next_row[:, 1:E], next_row[:, 0:E - 1], ALU.subtract).then_inc(s_link, 1)
            link(dve.tensor_tensor(t_base[:, :], t_f[:, 1:2], next_row[:, 0:1], ALU.add), 8)
            dve.scalar_tensor_tensor(move[:, :], n_tiles[:, :], float(P), move[:, :], ALU.mult, ALU.add).then_inc(s_link, 1)
            link(dve.tensor_scalar(past[:, :], cum[:, :], t_f[:, 0:1], None, ALU.is_le), 10)
            dve.tensor_reduce(t_expert[:, :], past[:, :], AX.X, ALU.add).then_inc(s_link, 1)
            link(dve.tensor_tensor(past_move[:, :], past[:, :], move[:, :], ALU.mult), 12)
            link(dve.tensor_reduce(t_row[:, :], past_move[:, :], AX.X, ALU.add), 13)
            dve.tensor_scalar(t_cols[:, 1:2], t_expert[:, :], float(E - 1), None, ALU.min).then_inc(s_cols, 1)
            dve.tensor_tensor(t_row[:, :], t_row[:, :], t_base[:, :], ALU.add).then_inc(s_cols, 1)
            dve.wait_ge(s_cols, 2)
            dve.tensor_scalar(t_cols[:, 0:1], t_row[:, :], float(E * REGION), None, ALU.min).then_inc(s_cols, 1)
            dve.wait_ge(s_tabT, 1)
            dve.tensor_copy(row_tab[:, :], psM[0:1, 0:P]).then_inc(s_row_tab, 1)
            link(dve.tensor_copy(packed[:, :], psM[0:1, P + PACK - 1:2 * P:PACK]), 14)
            for n in range(1, PACK):
                link(dve.scalar_tensor_tensor(packed[:, :], packed[:, :], float(SLOTS), psM[0:1, P + PACK - 1 - n:2 * P:PACK],
                                              ALU.mult, ALU.add), 14 + n)
            dve.tensor_copy(expert_tab[:, :], packed[:, :]).then_inc(s_tab, 1)

            def ffn(t, v, i, on, expert):
                if on[4]:
                    b2_at = dve.snap(expert(4) * D)
                if on[0]:
                    at = dve.snap(expert(0) * F)
                    if not (isinstance(t, int) and t < 4):
                        dve.wait_ge(f_w1, t - 3)
                    dve.tensor_copy(w1_tile[i % 4], w1_sb[:, bass.ds(at, F)]).then_inc(f_pick, 1)
                if on[4]:
                    r = (i - 4) % RING
                    o = 512 * (i % 2)
                    if not (isinstance(t, int) and t < 5):
                        dve.wait_ge(f_out, t - 4)
                    dve.wait_ge(f_w2, t - 3)
                    dve.tensor_tensor(ysum[:, :], psO[:, o:o + D], b2_sb[:, bass.ds(b2_at, D)], ALU.add).then_inc(f_sum, 1)
                    if not (isinstance(t, int) and t - 4 < RING):
                        dve.wait_ge(f_scat[r], 16 * (v + (i - 4) // RING))
                    dve.tensor_copy(tile_token[:, r:r + 1], tile_rows[r][:, ROW - 1:ROW].bitcast(I32))
                    dve.wait_ge(f_sum, t - 3)
                    dve.scalar_tensor_tensor(tile_out[r], ysum[:, :], tile_rows[r][:, 2 * D:2 * D + 1],
                                             tile_rows[r][:, 0:D], ALU.mult, ALU.add).then_inc(f_out, 1)

            dve.wait_ge(s_ffn, 32)
            dve.wait_ge(s_bias, 32)
            dve.wait_ge(s_tab, 1)
            ffn_run(dve, mybir.EngineType.DVE, ffn)


_INS = ['x', 'ctx_768', 'g_xattn', 'g_ffn', 'L0_xattn_g_x', 'L0_xattn_b_x', 'L0_xattn_g_c', 'L0_xattn_b_c',
        'L0_xattn_Wq', 'L0_xattn_Wk', 'L0_xattn_Wv', 'L0_xattn_Wo', 'L0_ffn_router_w', 'L0_ffn_w1', 'L0_ffn_b1',
        'L0_ffn_w2', 'L0_ffn_b2']


def kernel(**inputs):
    import numpy as _np
    import concourse.bacc as _bacc
    from concourse import mybir as _mybir
    from concourse.bass_utils import run_bass_kernel_spmd as _run

    nc = _bacc.Bacc("TRN2", target_bir_lowering=False, num_devices=1)
    arrays, args = {}, []
    for name in _INS:
        a = _np.ascontiguousarray(inputs[name])
        arrays[f"in_{name}_dram"] = a
        args.append(nc.dram_tensor(f"in_{name}_dram", a.shape, _mybir.dt.from_np(a.dtype), kind="ExternalInput").ap())
    shape = tuple(inputs['x'].shape)
    args.append(nc.dram_tensor("out_dram", shape, _mybir.dt.from_np(_np.dtype('float32')), kind="ExternalOutput").ap())
    gated_block_kernel(nc, *args)
    r = _run(nc, [arrays], core_ids=[0])
    return r.results[0]["out_dram"]
```
